# Optimizing a Trainium2 kernel written in Bass

```python
import numpy as np
import jax
import jax.numpy as jnp

def _softmax(x, axis=-1):
    return jax.nn.softmax(x, axis=axis)

def _gelu(x):
    return jax.nn.gelu(x, approximate=True)

def _silu(x):
    return jax.nn.silu(x)

def _sigmoid(x):
    return jax.nn.sigmoid(x)

def _layernorm(x, axis=-1, eps=1e-05):
    m = jnp.mean(x, axis=axis, keepdims=True)
    v = jnp.var(x, axis=axis, keepdims=True)
    return (x - m) / jnp.sqrt(v + eps)

def _scatter_add(tgt, idx, src, axis=0):
    return tgt.at[idx].add(src)

def _segment_sum(src, seg, n):
    return jax.ops.segment_sum(src, seg, n)
kernel_name = 'mk_sandwich_d1_jaxref_r4_2c6490'

def setup_inputs(seed: int=0):
    np.random.seed(seed)
    _w = jnp.asarray

    def _L0_attn_setup():
        import jax, jax.numpy as jnp
        import numpy as np
        H = 16
        KVH = 4
        D = 128
        HID = 512
        EPS = 1e-06
        GROUPS = H // KVH

        def elu_plus_one(x):
            return jax.nn.elu(x) + 1.0

        def _repeat_kv(x, b, s):
            x = x.reshape(b, s, KVH, 1, D)
            x = jnp.broadcast_to(x, (b, s, KVH, GROUPS, D))
            return x.reshape(b, s, H * D)

        def _split_heads(x, b, s, nh):
            return x.reshape(b, s, nh, D).transpose(0, 2, 1, 3)
        key = jax.random.key(seed)
        ks = jax.random.split(key, 8)
        s = 0.02
        return {'hidden_states': jax.random.normal(ks[0], (2, 1024, HID), jnp.float32), 'Wq': jax.random.normal(ks[1], (H * D, HID), jnp.float32) * s, 'bq': jnp.zeros((H * D,), jnp.float32), 'Wk': jax.random.normal(ks[2], (KVH * D, HID), jnp.float32) * s, 'bk': jnp.zeros((KVH * D,), jnp.float32), 'Wv': jax.random.normal(ks[3], (KVH * D, HID), jnp.float32) * s, 'bv': jnp.zeros((KVH * D,), jnp.float32), 'Wo': jax.random.normal(ks[4], (HID, H * D), jnp.float32) * s}
    _L0_attn_in = _L0_attn_setup()

    def _L0_ffn_setup():
        import jax, jax.numpy as jnp
        import numpy as np
        E = 32
        K = 8
        H = 512
        F = 192
        B, S = (1, 256)

        def _moe(x, wg, w1, v1, w2):
            T = x.shape[0]
            logits = x @ wg.T
            scores = jax.nn.softmax(logits, axis=-1)
            weights, idx = jax.lax.top_k(scores, K)
            weights = weights / jnp.sum(weights, axis=-1, keepdims=True)
            flat_e = idx.reshape(-1)
            flat_t = jnp.repeat(jnp.arange(T), K)
            flat_w = weights.reshape(-1)
            order = jnp.argsort(flat_e)
            e_s = flat_e[order]
            t_s = flat_t[order]
            w_s = flat_w[order]
            group_sizes = jnp.bincount(e_s, length=E).astype(jnp.int32)
            xs = x[t_s]
            g = jax.lax.ragged_dot(xs, w1, group_sizes)
            u = jax.lax.ragged_dot(xs, v1, group_sizes)
            h = jax.nn.silu(g) * u
            ys = jax.lax.ragged_dot(h, w2, group_sizes)
            out = jnp.zeros((T, x.shape[1]), x.dtype).at[t_s].add(ys * w_s[:, None])
            return out
        key = jax.random.key(seed)
        k0, k1, k2, k3, k4 = jax.random.split(key, 5)
        scale = 0.02
        return {'hidden_states': jax.random.normal(k0, (B, S, H), jnp.float32), 'wg': jax.random.normal(k1, (E, H), jnp.float32) * scale, 'w1': jax.random.normal(k2, (E, H, F), jnp.float32) * scale, 'v1': jax.random.normal(k3, (E, H, F), jnp.float32) * scale, 'w2': jax.random.normal(k4, (E, F, H), jnp.float32) * scale}
    _L0_ffn_in = _L0_ffn_setup()
    _d = {'L0_attn_hidden_states': _L0_attn_in['hidden_states'], 'L0_attn_Wq': _L0_attn_in['Wq'], 'L0_attn_bq': _L0_attn_in['bq'], 'L0_attn_Wk': _L0_attn_in['Wk'], 'L0_attn_bk': _L0_attn_in['bk'], 'L0_attn_Wv': _L0_attn_in['Wv'], 'L0_attn_bv': _L0_attn_in['bv'], 'L0_attn_Wo': _L0_attn_in['Wo'], 'L0_ffn_wg': _L0_ffn_in['wg'], 'L0_ffn_w1': _L0_ffn_in['w1'], 'L0_ffn_v1': _L0_ffn_in['v1'], 'L0_ffn_w2': _L0_ffn_in['w2']}
    _x0 = _d['L0_attn_hidden_states']
    _d['L0_attn_hidden_states'] = jax.random.normal(jax.random.fold_in(jax.random.key(seed), 1), (2, 2048, 512), dtype=_x0.dtype)
    del _x0
    return _d

def reference(L0_attn_hidden_states, L0_attn_Wq, L0_attn_bq, L0_attn_Wk, L0_attn_bk, L0_attn_Wv, L0_attn_bv, L0_attn_Wo, L0_ffn_wg, L0_ffn_w1, L0_ffn_v1, L0_ffn_w2):

    def _L0_attn_ref(hidden_states, Wq, bq, Wk, bk, Wv, bv, Wo):
        import jax, jax.numpy as jnp
        import numpy as np
        H = 16
        KVH = 4
        D = 128
        HID = 512
        EPS = 1e-06
        GROUPS = H // KVH

        def elu_plus_one(x):
            return jax.nn.elu(x) + 1.0

        def _repeat_kv(x, b, s):
            x = x.reshape(b, s, KVH, 1, D)
            x = jnp.broadcast_to(x, (b, s, KVH, GROUPS, D))
            return x.reshape(b, s, H * D)

        def _split_heads(x, b, s, nh):
            return x.reshape(b, s, nh, D).transpose(0, 2, 1, 3)
        b, s, _ = hidden_states.shape
        q = hidden_states @ Wq.T + bq
        k = hidden_states @ Wk.T + bk
        v = hidden_states @ Wv.T + bv
        k = _repeat_kv(k, b, s)
        v = _repeat_kv(v, b, s)
        q = _split_heads(q, b, s, H)
        k = _split_heads(k, b, s, H)
        v = _split_heads(v, b, s, H)
        sq = elu_plus_one(q)
        sk = elu_plus_one(k)
        kv = jnp.einsum('bhsd,bhse->bhde', sk, v)
        qkv = jnp.einsum('bhsd,bhde->bhse', sq, kv)
        k_sum = sk.sum(axis=2)
        norm = jnp.einsum('bhsd,bhd->bhs', sq, k_sum)
        attn = qkv / (norm[..., None] + EPS)
        attn = attn.transpose(0, 2, 1, 3).reshape(b, s, H * D)
        return attn @ Wo.T

    def _L0_ffn_ref(hidden_states, wg, w1, v1, w2):
        import jax, jax.numpy as jnp
        import numpy as np
        E = 32
        K = 8
        H = 512
        F = 192
        B, S = (1, 256)

        def _moe(x, wg, w1, v1, w2):
            T = x.shape[0]
            logits = x @ wg.T
            scores = jax.nn.softmax(logits, axis=-1)
            weights, idx = jax.lax.top_k(scores, K)
            weights = weights / jnp.sum(weights, axis=-1, keepdims=True)
            flat_e = idx.reshape(-1)
            flat_t = jnp.repeat(jnp.arange(T), K)
            flat_w = weights.reshape(-1)
            order = jnp.argsort(flat_e)
            e_s = flat_e[order]
            t_s = flat_t[order]
            w_s = flat_w[order]
            group_sizes = jnp.bincount(e_s, length=E).astype(jnp.int32)
            xs = x[t_s]
            g = jax.lax.ragged_dot(xs, w1, group_sizes)
            u = jax.lax.ragged_dot(xs, v1, group_sizes)
            h = jax.nn.silu(g) * u
            ys = jax.lax.ragged_dot(h, w2, group_sizes)
            out = jnp.zeros((T, x.shape[1]), x.dtype).at[t_s].add(ys * w_s[:, None])
            return out
        Bb, Ss, Hh = hidden_states.shape
        x = hidden_states.reshape(Bb * Ss, Hh)
        out = _moe(x, wg, w1, v1, w2)
        return out.reshape(Bb, Ss, Hh)
    x = L0_attn_hidden_states
    x = x + _layernorm(_L0_attn_ref(_layernorm(x, axis=-1), L0_attn_Wq, L0_attn_bq, L0_attn_Wk, L0_attn_bk, L0_attn_Wv, L0_attn_bv, L0_attn_Wo), axis=-1)
    x = x + _layernorm(_L0_ffn_ref(_layernorm(x, axis=-1), L0_ffn_wg, L0_ffn_w1, L0_ffn_v1, L0_ffn_w2), axis=-1)
    return x

_drawn_inputs = setup_inputs


def setup_inputs(seed=0):
    import zlib

    import numpy as np

    out = dict(_drawn_inputs(seed))
    spreads = {'L0_attn_bq': (0.0, 2.0), 'L0_attn_bk': (0.0, 2.0), 'L0_attn_bv': (0.0, 0.1)}
    factors = {'L0_attn_Wq': 9.963}
    for name, (base, spread) in spreads.items():
        noise = np.random.default_rng([zlib.crc32(name.encode()), seed]).standard_normal(out[name].shape)
        drawn = base * np.exp(spread * noise) if base else spread * noise
        out[name] = jnp.asarray(drawn.astype(out[name].dtype))
    for name, factor in factors.items():
        out[name] = (out[name] * factor).astype(out[name].dtype)
    return out
```

```python
import concourse.bass as bass
from concourse import mybir
from contextlib import ExitStack

BATCH, SEQ, HID = 2, 2048, 512
HEADS, KV_HEADS, HEAD_DIM = 16, 4, 128
EXPERTS, TOP_K, FFN = 32, 8, 192
P = 128
TOKENS = BATCH * SEQ
TILES = TOKENS // P
BATCH_TILES = SEQ // P
KC = HID // P
GROUP = HEADS // KV_HEADS
CHUNKS = HEADS // GROUP
ATTN_EPS, NORM_EPS = 1e-6, 1e-5

W_COL, ROW = HID, HID + EXPERTS
PAIR = 2 * P
CAP = TOKENS + PAIR
COLS = CAP // P
TRASH = TOKENS

UP = 2 * FFN
W13 = KC * UP
W2H, W2L, W2X = 2 * W13, 2 * W13 + HID, 2 * W13 + 2 * HID
WSET = 2 * W13 + 3 * HID
WSETS = 4
RING = 4
RAW_N = W13 + 2 * HID


def layer(nc, x_in, wkv_in, bq_in, bkv_in, wq_in, wo_in, wg_in, w13_in, w2_in, out):
    f32, f32r, i32, u32 = mybir.dt.float32, mybir.dt.float32r, mybir.dt.int32, mybir.dt.uint32
    ALU, ACT, AX = mybir.AluOpType, mybir.ActivationFunctionType, mybir.AxisListType

    lists = nc.dram_tensor("expert_lists", (EXPERTS * CAP, 1), i32, kind="Internal").ap()
    rows_dram = nc.dram_tensor("token_rows", (TOKENS + PAIR, ROW), f32, kind="Internal").ap()
    acc_dram = nc.dram_tensor("moe_sum", (TOKENS + PAIR, HID), f32, kind="Internal").ap()
    x2_dram = nc.dram_tensor("after_attention", (TOKENS, HID), f32, kind="Internal").ap()

    ctx = ExitStack()
    with ctx:
        def sb(name, shape, dt=f32):
            return ctx.enter_context(nc.sbuf_tensor(name, shape, dt))

        def sem(name):
            return ctx.enter_context(nc.semaphore(name))

        def wait(eng, s, v):
            if not (isinstance(v, int) and v <= 0):
                eng.wait_ge(s, v)

        def stand(eng):
            eng.sem_inc(s_stood, 1)

        WB = sb("WB", [P, 2 * KC * HEADS * HEAD_DIM + 2 * HEADS * HID], f32r)
        NQ, NM = KC * HEADS * HEAD_DIM, HEADS * HID
        wq_hi = WB[:, 0:NQ]
        wq_lo = WB[:, NQ:2 * NQ]
        m_hi = WB[:, 2 * NQ:2 * NQ + NM]
        m_lo = WB[:, 2 * NQ + NM:2 * NQ + 2 * NM]
        wkv_hi = m_hi[:, 0:KC * 2 * HID]
        wkv_lo = m_lo[:, 0:KC * 2 * HID]
        XH = sb("XH", [P, 2, KC, P], f32r)
        XL = sb("XL", [P, 2, KC, P], f32r)
        SH = sb("SH", [P, 2, GROUP, P], f32r)
        SL = sb("SL", [P, 2, GROUP, P], f32r)
        RAW = sb("RAW", [P, RAW_N])
        raw2 = [RAW[:, 1024 * i:1024 * (i + 1)] for i in range(2)]
        X = sb("X", [P, 2, HID])
        XN = sb("XN", [P, HID])
        XRES = sb("XRES", [P, 2, HID])
        BIG = sb("BIG", [P, 5120])
        bkv = BIG[:, 0:1024]
        zk = BIG[:, 1024:1536]
        ek = BIG[:, 1536:2048]
        sk = BIG[:, 2048:3072].rearrange("p (i n) -> p i n", i=2)
        vx = BIG[:, 3072:3072 + 2 * KV_HEADS * (HEAD_DIM + 2)].rearrange("p (i h n) -> p i h n", i=2, h=KV_HEADS)
        z = BIG[:, 0:1024].rearrange("p (i n) -> p i n", i=2)
        e = BIG[:, 1024:2048].rearrange("p (i n) -> p i n", i=2)
        sq = BIG[:, 2048:3072].rearrange("p (i n) -> p i n", i=2)
        sqn = BIG[:, 3072:4096].rearrange("p (i n) -> p i n", i=2)
        prod = BIG[:, 4096:4608]
        on = BIG[:, 4608:5120]
        xr = BIG[:, 0:2 * ROW].rearrange("p (i n) -> p i n", i=2)
        o = 2 * ROW
        sg = BIG[:, o:o + 2 * FFN].rearrange("p (i n) -> p i n", i=2)
        o += 2 * FFN
        hx = BIG[:, o:o + 2 * 2 * P].rearrange("p (i n) -> p i n", i=2)
        o += 4 * P
        wring = BIG[:, o:o + 2 * RING * EXPERTS].rearrange("p (i r n) -> p i r n", i=2, r=RING)
        yb = X
        bq = sb("bq", [P, HEADS * HEAD_DIM])
        row = sb("row", [P, 2, ROW])
        kvs0 = sb("kvs0", [P, KV_HEADS * (HEAD_DIM + 1)])
        kvs1 = sb("kvs1", [P, KV_HEADS * (HEAD_DIM + 1)])
        kvs = [t[:, :].rearrange("p (h n) -> p h n", h=KV_HEADS) for t in (kvs0, kvs1)]
        kvt = kvs0[:, 0:HID].rearrange("p (h n) -> p h n", h=KV_HEADS)
        x2t = kvt
        ksum1 = sb("ksum1", [P, HID])
        ksumb = [RAW[:, 2048:2048 + HID], ksum1]
        ident = sb("ident", [P, P])
        ones = sb("ones", [P, P])
        upper = sb("upper", [P, P])
        zero = on
        wg = sb("wg", [P, KC, EXPERTS])
        iota_e = sb("iota_e", [P, EXPERTS])
        carry = sb("carry", [P, EXPERTS])
        idf = sb("idf", [P, 1])
        bst = sb("bst", [P, 3, 6])
        mv = sb("mv", [P, 3, 2])
        ve = sb("ve", [P, 3])
        rs = sb("rs", [P, 3])
        mhalf = sb("mhalf", [P, 1])
        mhalf2 = sb("mhalf2", [P, 2])
        nmr = sb("nmr", [P, 1])
        nrm = sb("nrm", [P, GROUP])
        nre = sb("nre", [P, GROUP])
        rec = sb("rec", [P, 2, GROUP])
        lg = sb("lg", [P, EXPERTS])
        mx8 = sb("mx8", [P, TOP_K])
        ix8 = sb("ix8", [P, TOP_K], u32)
        ixf = sb("ixf", [P, TOP_K])
        negmax = sb("negmax", [P, 1])
        ex = sb("ex", [P, EXPERTS])
        oh = sb("oh", [P, TOP_K, EXPERTS])
        msk = sb("msk", [P, EXPERTS])
        wun = sb("wun", [P, EXPERTS])
        wsum = sb("wsum", [P, 1])
        wrec = sb("wrec", [P, 1])
        rank = sb("rank", [P, EXPERTS])
        posf = sb("posf", [P, TOP_K])
        pos = sb("pos", [P, 2, TOP_K], u32)
        cnt_f, cnt_i, pr_i, pr_f, inc_f = [oh[0:1, i, :] for i in range(5)]
        cnt_i, pr_i = cnt_i.bitcast(i32), pr_i.bitcast(i32)
        table = sb("table", [1, 2, EXPERTS], i32)
        rank_i = sb("rank_i", [P, TOP_K], i32)
        col_i = sb("col_i", [P, TOP_K], i32)
        col_f = sb("col_f", [P, TOP_K])
        at_f = sb("at_f", [P, TOP_K])
        ids = sb("ids", [P, 2, 1], i32)
        lst = sb("lst", [P, 2, COLS], i32)
        gidx = sb("gidx", [P, 2], i32)
        aidx = sb("aidx", [P, 2], i32)
        idring = sb("idring", [P, 2, RING], i32)
        trash = bq[:, 0:EXPERTS * COLS].bitcast(i32)

        bank = [ctx.enter_context(nc.psum_tensor(f"bank{i}", [P, HID], f32)) for i in range(8)]
        pt, pk, pv, pkv, pr = bank[0], bank[1:3], bank[3:5], bank[5:7], bank[7]
        pq, pst, po = bank[1:3], bank[3:5], bank[5:7]
        et, eu, eh, ed = [bank[0], bank[7]], bank[1:3], bank[3:5], bank[5:7]

        s_stood = sem("stood")
        s_const, s_consts2, s_bias, s_wg = sem("const"), sem("const_pool"), sem("bias_loaded"), sem("wg_loaded")
        s_zero, s_zeroed = sem("zero_ready"), sem("sum_zeroed")
        s_trash, s_lists = sem("padding_ids"), sem("lists_filled")
        s_raw = [sem("raw_loaded0"), sem("raw_loaded1")]
        s_whi, s_wlo = sem("weights_high"), sem("weights_low")
        s_x = [sem("x_loaded0"), sem("x_loaded1")]
        s_bs, s_mv, s_ve, s_rs, s_xn = sem("x_stats"), sem("x_meanvar"), sem("x_var_eps"), sem("x_rstd"), sem("x_norm")
        s_xt, s_xh, s_xl = sem("x_transposed"), sem("x_high"), sem("x_low")
        s_k, s_v, s_z, s_nr, s_e = sem("k_done"), sem("v_done"), sem("zk"), sem("zk_neg"), sem("zk_exp")
        s_sk, s_vx, s_acc, s_kvev = sem("sk"), sem("vx"), sem("kv_added"), sem("kv_evacuated")
        s_diag, s_ksb, s_ksum = sem("ksum_diag"), sem("ksum_spread"), sem("ksum_ready")
        s_q, s_zq, s_nq, s_eq, s_sq = sem("q_done"), sem("zq"), sem("zq_neg"), sem("zq_exp"), sem("sq")
        s_prod, s_red, s_eps, s_rec, s_scale = sem("prod"), sem("norm_sum"), sem("norm_eps"), sem("norm_rec"), sem("scaled")
        s_st, s_shi, s_slo, s_o = sem("s_transposed"), sem("s_high"), sem("s_low"), sem("o_chunk")
        s_kt, s_ktc, s_m, s_mhi, s_mlo = sem("kv_transposed"), sem("kvt_copied"), sem("m_done"), sem("m_high"), sem("m_low")
        s_xres = [sem("xres_loaded0"), sem("xres_loaded1")]
        s_x2st = [sem("x2_stored0"), sem("x2_stored1")]
        s_obs, s_omv, s_ove, s_ors, s_nmr, s_on = (sem("o_stats"), sem("o_meanvar"), sem("o_var_eps"), sem("o_rstd"),
                                                   sem("o_shift"), sem("o_norm"))
        s_x2, s_2bs, s_2mv, s_2ve, s_2rs, s_row = (sem("x2"), sem("x2_stats"), sem("x2_meanvar"), sem("x2_var_eps"),
                                                   sem("x2_rstd"), sem("row"))
        s_rt, s_x2t, s_lgt, s_lg, s_mx, s_nmx, s_ix, s_ixf = (sem("x2_transposed"), sem("x2t"), sem("logits"), sem("lg"),
                                                              sem("mx8"), sem("negmax"), sem("ix8"), sem("ixf"))
        s_oh, s_msk, s_ex, s_rank, s_rk = sem("one_hot"), sem("mask"), sem("ex"), sem("rank_done"), sem("rank")
        s_wun, s_wsum, s_wrec, s_wd, s_pf, s_pos = (sem("w_raw"), sem("w_sum"), sem("w_rec"), sem("w_row"),
                                                    sem("pos_prod"), sem("pos"))
        s_posf, s_ri, s_ci, s_cf, s_id = sem("posf"), sem("rank_int"), sem("col_int"), sem("col_float"), sem("id_col")
        s_sc = [sem("ids_sent0"), sem("ids_sent1")]
        s_rst = [sem("row_stored0"), sem("row_stored1")]
        s_tab, s_tabd = sem("table_steps"), sem("table_ready")
        s_ewr, s_ehi, s_elo = sem("ew_loaded"), sem("ew_high"), sem("ew_low")
        s_pad, s_pad0 = sem("zero_pair_ready"), sem("padding_zeros")
        s_lst, s_lused = [sem("list_loaded0"), sem("list_loaded1")], sem("list_used")
        two = lambda name: [sem(f"{name}_{i}") for i in "AB"]
        s_ld = two("rows_loaded")
        s_T, s_exh, s_exl = two("e_transposed"), two("e_high"), two("e_low")
        s_U, s_sg, s_h = two("e_up"), two("e_silu"), two("e_act")
        s_H, s_hh, s_hl = two("e_act_transposed"), two("e_act_high"), two("e_act_low")
        s_D, s_y, s_add = two("e_down"), two("e_out"), two("e_added")
        s_gi, s_ai = two("gather_index"), two("add_index")
        s_fl = [sem("f_loaded0"), sem("f_loaded1")]
        s_fst = [sem("f_stored0"), sem("f_stored1")]
        s_fbs, s_fmv, s_fve, s_frs, s_fnm, s_fn, s_fo = (sem("f_stats"), sem("f_meanvar"), sem("f_var_eps"), sem("f_rstd"),
                                                         sem("f_shift"), sem("f_norm"), sem("f_out"))

        block = ctx.enter_context(nc.Block())

        def pairs_of(lo, hi, eng, body):
            with eng.Fori(lo // 2, hi // 2) as p:
                body(2 * p, 0)
                body(2 * p + 1, 1)

        A_PLAN = [(0, 2), (2, 16), (16, 18), (18, 32)]
        B_PLAN = [(0, 4), (4, 16), (16, 18), (18, 30), (30, 36)]

        def run_a(eng, body):
            for lo, hi in A_PLAN:
                if hi - lo > 6:
                    pairs_of(lo, hi, eng, body)
                else:
                    for u in range(lo, hi):
                        body(u, u % 2)

        def run_b(eng, body):
            for lo, hi in B_PLAN:
                if hi - lo > 6:
                    pairs_of(lo, hi, eng, lambda t, s, b=lo // BATCH_TILES: body(t, s, b))
                else:
                    for t in range(lo, hi):
                        body(t, t % 2, min(t // BATCH_TILES, 1))

        def live(t, lag=0):
            return not isinstance(t, int) or 0 <= t - lag < TILES

        def each_expert(eng, body):
            eng.wait_ge(s_tabd, 1)

            def one(e, q):
                n = eng.value_load(table[0:1, 0, bass.ds(e, 1)], min_val=1, max_val=TOKENS // PAIR)
                first = eng.value_load(table[0:1, 1, bass.ds(e, 1)], min_val=0, max_val=EXPERTS * TOKENS // PAIR)
                body(e, q, first, n)
                return first + n

            with eng.Fori(0, EXPERTS // WSETS - 1) as r:
                for q in range(WSETS):
                    one(r * WSETS + q, q)
            for e in range(EXPERTS - WSETS, EXPERTS):
                total = one(e, e % WSETS)
            return total

        def slot_of(g):
            return (g + RING) & (RING - 1)

        def moe_sp(sp):
            def load_weights(e):
                sp.dma_start(RAW[:, 0:W13], w13_in[bass.ds(e, 1), :, :].rearrange("a p n -> p (a n)")).then_inc(s_ewr, 16)
                sp.dma_start(RAW[:, W13:W13 + HID], w2_in[bass.ds(e, 1), 0:P, :].rearrange("a p n -> p (a n)")).then_inc(s_ewr, 16)
                for i in range(2):
                    sp.dma_start(RAW[i * 64:(i + 1) * 64, W13 + HID:RAW_N],
                                 w2_in[bass.ds(e, 1), P:FFN, :].rearrange("a p n -> p (a n)")).then_inc(s_ewr, 16)

            def load_list(e, i):
                sp.dma_start(lst[:, i, :], lists[bass.ds(e * CAP, CAP), :].rearrange("(p q) a -> p (q a)", p=P)).then_inc(s_lst[i], 16)

            sp.wait_ge(s_m, BATCH * HEADS)
            load_weights(0)
            sp.wait_ge(s_elo, 1)
            load_weights(1)
            for i in range(2):
                sp.wait_ge(s_sc[i], TILES // 2 * TOP_K * 16)
            load_list(0, 0)
            load_list(1, 1)

            def body(e, i):
                sp.wait_ge(s_lused, e + 1)
                stand(sp)
                load_list(e + 2, i)
                sp.wait_ge(s_elo, e + 2)
                stand(sp)
                load_weights(e + 2)

            with sp.Fori(0, EXPERTS // 2 - 1) as r:
                body(2 * r, 0)
                body(2 * r + 1, 1)

            sp.wait_ge(s_tabd, 1)
            total = (sp.value_load(table[0:1, 1, EXPERTS - 1:EXPERTS], min_val=0, max_val=EXPERTS * TOKENS // PAIR)
                     + sp.value_load(table[0:1, 0, EXPERTS - 1:EXPERTS], min_val=1, max_val=TOKENS // PAIR))
            sp.wait_ge(s_T[0], total + 2)
            for i in range(2):
                sp.wait_ge(s_add[i], 16 * total + 48 + 16 * i)
                stand(sp)
                sp.wait_ge(s_x2st[i], 16 * (TILES // 2))

            def load(f, r):
                rows = bass.ds(f * PAIR, PAIR)
                sp.dma_start(fa[:, r, :, :], acc_dram[rows, :].rearrange("(j p) n -> p j n", p=P)).then_inc(s_fl[r], 16)
                sp.dma_start(fx[:, r, :, :], x2_dram[rows, :].rearrange("(j p) n -> p j n", p=P)).then_inc(s_fl[r], 16)

            def step(f, r, more):
                sp.wait_ge(s_fo, f + 1)
                sp.dma_start(out[bass.ds(f * PAIR, PAIR), :].rearrange("(j p) n -> p j n", p=P), fx[:, r, :, :]).then_inc(s_fst[r], 16)
                if more:
                    sp.wait_ge(s_fst[r], (f - r) * 8 + 16)
                    load(f + 2, r)

            load(0, 0)
            load(1, 1)
            with sp.Fori(0, TILES // 4 - 1) as p:
                step(2 * p, 0, True)
                step(2 * p + 1, 1, True)
            step(TILES // 2 - 2, 0, False)
            step(TILES // 2 - 1, 1, False)
            for r in range(2):
                sp.wait_ge(s_fst[r], 16 * (TILES // 4))

        fa = BIG[:, 0:2048].rearrange("p (r j n) -> p r j n", r=2, j=2)
        fx = BIG[:, 2048:4096].rearrange("p (r j n) -> p r j n", r=2, j=2)
        fmv = sb("fmv", [P, 2, 2])
        fve = sb("fve", [P, 2])
        frs = sb("frs", [P, 2])
        fnm = sb("fnm", [P, 2])

        def moe_pe(pe):
            for s in range(2):
                for x in (s_T, s_U, s_D):
                    pe.sem_inc(x[s], 1)
                pe.sem_inc(s_H[s], 2 - s)

            def rows_t(g, s):
                pe.wait_ge(s_ld[s], 16 * g + 16)
                pe.wait_ge(s_exl[s], g + 1)
                for k in range(KC):
                    last = nc.tensor.transpose(et[s][:, k * P:(k + 1) * P], xr[:, s, k * P:(k + 1) * P], ident[:, :])
                last.then_inc(s_T[s], 1)

            def up(g, s, q):
                pe.wait_ge(s_exl[s], g + 2)
                pe.wait_ge(s_h[s], g + 1)
                w = WB[:, q * WSET:(q + 1) * WSET]
                for k in range(KC):
                    wh, wl = w[:, k * UP:(k + 1) * UP], w[:, W13 + k * UP:W13 + (k + 1) * UP]
                    nc.tensor.matmul(eu[s][:, 0:UP], XL[:, s, k, :], wh, start=k == 0, stop=False)
                    nc.tensor.matmul(eu[s][:, 0:UP], XH[:, s, k, :], wl, start=False, stop=False)
                    last = nc.tensor.matmul(eu[s][:, 0:UP], XH[:, s, k, :], wh, start=False, stop=k == KC - 1)
                last.then_inc(s_U[s], 1)

            def act_t(g, s):
                pe.wait_ge(s_h[s], g + 2)
                pe.wait_ge(s_hl[s], g + 2)
                for c in range(2):
                    last = nc.tensor.transpose(eh[s][:, c * P:(c + 1) * P], hx[:, s, c * P:(c + 1) * P], ident[:, :])
                last.then_inc(s_H[s], 1)

            def down(g, s, at):
                pe.wait_ge(s_hl[s], g + 3)
                pe.wait_ge(s_y[s], g + 3)
                w = lambda o: WB[:, bass.ds(at + o, HID)]
                nc.tensor.matmul(ed[s][:, :], SL[:, s, 0, :], w(W2H), start=True, stop=False)
                nc.tensor.matmul(ed[s][:, :], SH[:, s, 0, :], w(W2L), start=False, stop=False)
                nc.tensor.matmul(ed[s][:, :], SH[:, s, 0, :], w(W2H), start=False, stop=False)
                nc.tensor.matmul(ed[s][:, :], SL[0:64, s, 1, :], WB[0:64, bass.ds(at + W2X, HID)], start=False, stop=False)
                nc.tensor.matmul(ed[s][:, :], SH[:, s, 1, :], w(W2X), start=False, stop=True).then_inc(s_D[s], 1)

            rows_t(0, 0)

            def body(e, q, first, n):
                pe.wait_ge(s_elo, e + 1)
                stand(pe)
                with pe.Fori(0, n) as i:
                    g = first + i
                    back = (WSETS - 1) * WSET if q == 0 else -WSET
                    prev = pe.snap(q * WSET + back - ((i + TOKENS - 1) // TOKENS) * back)
                    rows_t(g, 1)
                    up(g, 0, q)
                    act_t(g - 1, 1)
                    down(g - 1, 0, prev)
                    rows_t(g + 1, 0)
                    up(g, 1, q)
                    act_t(g, 0)
                    down(g - 1, 1, prev)

            total = each_expert(pe, body)
            last = (EXPERTS - 1) % WSETS * WSET
            act_t(total - 1, 1)
            down(total - 1, 0, last)
            down(total - 1, 1, last)

        def moe_act(act):
            for s in range(2):
                for x in (s_exh, s_sg):
                    act.sem_inc(x[s], 1)
                act.sem_inc(s_y[s], 2)
                act.sem_inc(s_hh[s], 2 - s)

            def weights_high(e, q):
                act.wait_ge(s_ewr, 64 * e + 64)
                w = WB[:, q * WSET:(q + 1) * WSET]
                nc.scalar.activation(w[:, 0:W13], RAW[:, 0:W13], ACT.Copy)
                nc.scalar.activation(w[:, W2H:W2H + HID], RAW[:, W13:W13 + HID], ACT.Copy)
                nc.scalar.activation(w[:, W2X:W2X + HID], RAW[:, W13 + HID:RAW_N], ACT.Copy).then_inc(s_ehi, 1)

            def rows_high(g, s):
                act.wait_ge(s_T[s], g + 2)
                act.wait_ge(s_U[s], g + 1)
                nc.scalar.activation(XH[:, s, :, :].rearrange("p k n -> p (k n)"), et[s][:, :], ACT.Copy).then_inc(s_exh[s], 1)

            def silu(g, s):
                act.wait_ge(s_U[s], g + 2)
                act.wait_ge(s_h[s], g + 1)
                nc.scalar.activation(sg[:, s, :], eu[s][:, 0:FFN], ACT.Silu).then_inc(s_sg[s], 1)

            def act_high(g, s):
                act.wait_ge(s_H[s], g + 3)
                act.wait_ge(s_D[s], g + 2)
                nc.scalar.activation(SH[:, s, 0:2, :].rearrange("p k n -> p (k n)"), eh[s][:, 0:2 * P], ACT.Copy).then_inc(s_hh[s], 1)

            def weigh(g, s, e):
                act.wait_ge(s_D[s], g + 3)
                act.wait_ge(s_add[s], 16 * (g + 3 + s))
                act.wait_ge(s_exl[s], g + 2)
                w = wring[:, s, bass.ds(slot_of(g), 1), bass.ds(e, 1)].rearrange("p a n -> p (a n)")
                nc.scalar.activation(yb[:, s, :], ed[s][:, :], ACT.Copy, scale=w).then_inc(s_y[s], 1)

            act.wait_ge(s_q, 4 * TILES)
            weights_high(0, 0)
            act.wait_ge(s_pad, 1)
            rows_high(0, 0)

            def body(e, q, first, n):
                if not (isinstance(e, int) and e + 1 == EXPERTS):
                    weights_high(e + 1, (q + 1) % WSETS)
                with act.Fori(0, n) as i:
                    g = first + i
                    eb = act.snap((e + EXPERTS - 1 + (i + TOKENS - 1) // TOKENS) & (EXPERTS - 1))
                    rows_high(g, 1)
                    silu(g, 0)
                    act_high(g - 1, 1)
                    weigh(g - 1, 0, eb)
                    rows_high(g + 1, 0)
                    silu(g, 1)
                    act_high(g, 0)
                    weigh(g - 1, 1, eb)

            total = each_expert(act, body)
            act_high(total - 1, 1)
            weigh(total - 1, 0, EXPERTS - 1)
            weigh(total - 1, 1, EXPERTS - 1)

            def step(f, r):
                act.wait_ge(s_fnm, f + 1)
                for j in range(2):
                    last = nc.scalar.activation(fa[:, r, j, :], fa[:, r, j, :], ACT.Identity, bias=fnm[:, j:j + 1],
                                                scale=frs[:, j:j + 1])
                last.then_inc(s_fn, 1)

            with act.Fori(0, TILES // 4) as p:
                step(2 * p, 0)
                step(2 * p + 1, 1)

        def moe_dve(dve):
            dve.wait_ge(s_rk, 2 * TILES)
            dve.wait_ge(s_posf, TILES)
            nc.vector.tensor_copy(cnt_f, carry[0:1, :]).then_inc(s_tab, 1)
            dve.wait_ge(s_tab, 1)
            nc.vector.tensor_scalar(cnt_i, cnt_f, float(PAIR - 1), None, ALU.add).then_inc(s_tab, 1)
            dve.wait_ge(s_tab, 2)
            nc.vector.tensor_scalar(pr_i, cnt_i, PAIR.bit_length() - 1, None, ALU.arith_shift_right).then_inc(s_tab, 1)
            dve.wait_ge(s_tab, 3)
            nc.vector.tensor_scalar(pr_f, pr_i, 1.0, None, ALU.max).then_inc(s_tab, 1)
            nc.vector.memset(cnt_f, 0.0).then_inc(s_tab, 1)
            dve.wait_ge(s_tab, 5)
            nc.vector.tensor_copy(table[:, 0, :], pr_f)
            nc.vector.tensor_tensor_scan(inc_f, pr_f, cnt_f, 0.0, ALU.add, ALU.add).then_inc(s_tab, 1)
            dve.wait_ge(s_tab, 6)
            nc.vector.tensor_tensor(table[:, 1, :], inc_f, pr_f, ALU.subtract).then_inc(s_tabd, 1)
            dve.wait_ge(s_o, 4 * TILES)
            nc.vector.memset(SH[:, 0, 0:2, :].bitcast(f32), 0.0)
            nc.vector.memset(SL[:, 0, 0:2, :].bitcast(f32), 0.0)
            nc.vector.memset(WB[:, (WSETS - 1) * WSET + W2H:WSETS * WSET].bitcast(f32), 0.0)
            nc.vector.memset(hx[:, 1, :], 0.0).then_inc(s_tab, 1)
            dve.wait_ge(s_tab, 7)
            for s in range(2):
                for x in (s_exl, s_h):
                    dve.sem_inc(x[s], 1)
                dve.sem_inc(s_hl[s], 2 - s)

            def weights_low(e, q):
                dve.wait_ge(s_ehi, e + 1)
                w = WB[:, q * WSET:(q + 1) * WSET]
                nc.vector.tensor_tensor(w[:, W13:2 * W13], RAW[:, 0:W13], w[:, 0:W13].bitcast(f32), ALU.subtract)
                nc.vector.tensor_tensor(w[:, W2L:W2L + HID], RAW[:, W13:W13 + HID], w[:, W2H:W2H + HID].bitcast(f32), ALU.subtract)
                low = w[64:P, W2X:W2X + HID]
                nc.vector.tensor_tensor(low, RAW[64:P, W13 + HID:RAW_N], low.bitcast(f32), ALU.subtract).then_inc(s_elo, 1)

            def rows_low(g, s):
                dve.wait_ge(s_exh[s], g + 2)
                nc.vector.tensor_copy(wring[:, s, bass.ds(slot_of(g), 1), :].rearrange("p a n -> p (a n)"), xr[:, s, W_COL:ROW])
                hi = XH[:, s, :, :].rearrange("p k n -> p (k n)")
                nc.vector.tensor_tensor(XL[:, s, :, :].rearrange("p k n -> p (k n)"), et[s][:, :], hi.bitcast(f32),
                                        ALU.subtract).then_inc(s_exl[s], 1)

            def gate(g, s):
                dve.wait_ge(s_sg[s], g + 2)
                dve.wait_ge(s_H[s], g + 2)
                nc.vector.tensor_tensor(hx[:, s, 0:P], sg[:, s, 0:P], eu[s][:, FFN:FFN + P], ALU.mult)
                shape, twice = (P, 2, FFN - P), "p (a n) -> p a n"
                nc.vector.tensor_tensor(hx[:, s, P:2 * P].rearrange(twice, a=2),
                                        sg[:, s, P:FFN].rearrange(twice, a=1).to_broadcast(shape),
                                        eu[s][:, FFN + P:UP].rearrange(twice, a=1).to_broadcast(shape), ALU.mult).then_inc(s_h[s], 1)

            def act_low(g, s):
                dve.wait_ge(s_hh[s], g + 3)
                hi = SH[:, s, 0:2, :].rearrange("p k n -> p (k n)")
                nc.vector.tensor_tensor(SL[:, s, 0:2, :].rearrange("p k n -> p (k n)"), eh[s][:, 0:2 * P], hi.bitcast(f32),
                                        ALU.subtract).then_inc(s_hl[s], 1)

            weights_low(0, 0)

            def body(e, q, first, n):
                if not (isinstance(e, int) and e + 1 == EXPERTS):
                    weights_low(e + 1, (q + 1) % WSETS)
                with dve.Fori(0, n) as i:
                    g = first + i
                    rows_low(g, 1)
                    gate(g, 0)
                    act_low(g - 1, 1)
                    rows_low(g + 1, 0)
                    gate(g, 1)
                    act_low(g, 0)

            rows_low(0, 0)
            total = each_expert(dve, body)
            act_low(total - 1, 1)

            def stats(f, r):
                dve.wait_ge(s_fl[r], (f - r) * 16 + 32)
                for j in range(2):
                    nc.vector.bn_stats(bst[:, j, :], fa[:, r, j, :]).then_inc(s_fbs, 1)
                for j in range(2):
                    dve.wait_ge(s_fbs, 2 * f + 1 + j)
                    stand(dve)
                    nc.vector.bn_aggr(fmv[:, j, :], bst[:, j, :]).then_inc(s_fmv, 1)

            def shift(f):
                dve.wait_ge(s_frs, f + 1)
                nc.vector.scalar_tensor_tensor(fnm[:, :], fmv[:, :, 0], -1.0, frs[:, :], ALU.mult, ALU.mult).then_inc(s_fnm, 1)

            def add(f, r):
                dve.wait_ge(s_fn, f + 1)
                nc.vector.tensor_tensor(fx[:, r, :, :], fx[:, r, :, :], fa[:, r, :, :], ALU.add).then_inc(s_fo, 1)

            stats(0, 0)
            shift(0)
            stats(1, 1)
            add(0, 0)
            shift(1)
            with dve.Fori(1, TILES // 4) as p:
                stats(2 * p, 0)
                add(2 * p - 1, 1)
                shift(2 * p)
                stats(2 * p + 1, 1)
                add(2 * p, 0)
                shift(2 * p + 1)
            add(TILES // 2 - 1, 1)

        def moe_pool(pool):
            for i in range(2):
                pool.wait_ge(s_sc[i], TILES // 2 * TOP_K * 16)
                pool.wait_ge(s_rst[i], TILES // 2 * 16)
            pool.wait_ge(s_xn, 2 * TILES)
            nc.gpsimd.memset(wring, 0.0).then_inc(s_pad, 1)
            for s in range(2):
                nc.gpsimd.memset(yb[:, s, :], 0.0).then_inc(s_pad0, 1)
                nc.gpsimd.iota(idring[:, s, :], [[0, RING]], base=TRASH + s * P, channel_multiplier=1).then_inc(s_pad0, 1)
                nc.gpsimd.iota(aidx[:, s:s + 1], [[0, 1]], base=TRASH + s * P, channel_multiplier=1).then_inc(s_pad0, 1)
            pool.wait_ge(s_pad0, 6)

            def add_rows(s):
                nc.gpsimd.indirect_dma_start(acc_dram[:, :], bass.IndirectOffsetOnAxis(aidx[:, s:s + 1], 0), yb[:, s, :], None,
                                             compute_op=ALU.add).then_inc(s_add[s], 16)

            for s in range(2):
                add_rows(s)

            def add(g, s):
                pool.wait_ge(s_y[s], g + 4)
                if s == 0:
                    pool.wait_ge(s_add[0], 16 * (g + 3))
                pool.wait_ge(s_add[1], 16 * (g + 4))
                nc.gpsimd.tensor_copy(aidx[:, s:s + 1], idring[:, s, bass.ds(slot_of(g), 1)]).then_inc(s_ai[s], 1)
                pool.wait_ge(s_ai[s], g + 3 + s)
                stand(pool)
                add_rows(s)

            def gather(g, s, q, col):
                pool.wait_ge(s_exl[s], g + 1)
                src = lst[:, q, bass.ds(col, 1)]
                nc.gpsimd.tensor_copy(idring[:, s, bass.ds(slot_of(g), 1)], src)
                nc.gpsimd.tensor_copy(gidx[:, s:s + 1], src).then_inc(s_gi[s], 1)
                pool.wait_ge(s_gi[s], g + 1)
                stand(pool)
                nc.gpsimd.indirect_dma_start(xr[:, s, :], None, rows_dram[:, :], bass.IndirectOffsetOnAxis(gidx[:, s:s + 1], 0)
                                             ).then_inc(s_ld[s], 16)

            def body(e, q, first, n):
                pool.wait_ge(s_lst[q % 2], (e - q % 2) * 8 + 16)
                stand(pool)
                with pool.Fori(0, n) as i:
                    g = first + i
                    gather(g, 0, q % 2, 2 * i)
                    add(g - 3, 1)
                    gather(g, 1, q % 2, 2 * i + 1)
                    add(g - 2, 0)
                pool.sem_inc(s_lused, 1)

            total = each_expert(pool, body)
            gather(total, 0, 1, COLS - 1)
            add(total - 3, 1)
            for g in (total - 2, total - 1):
                add(g, 0)
                add(g, 1)

            def frstd(f):
                pool.wait_ge(s_fmv, 2 * f + 2)
                stand(pool)
                nc.gpsimd.tensor_scalar(fve[:, :], fmv[:, :, 1], NORM_EPS, None, ALU.add).then_inc(s_fve, 1)
                pool.wait_ge(s_fve, f + 1)
                nc.gpsimd.tensor_tensor(frs[:, :], fve[:, :], mhalf2[:, :], ALU.pow).then_inc(s_frs, 1)

            frstd(0)
            with pool.Fori(1, TILES // 2) as f:
                pool.wait_ge(s_fn, f)
                frstd(f)


        @block.sync
        def _(sp):
            x_tiles = x_in.rearrange("(t p) n -> p t n", p=P)

            def load_x(u, s, t):
                wait(sp, s_xn, u - 1)
                sp.dma_start(X[:, s, :], x_in[bass.ds(t * P, P), :]).then_inc(s_x[s], 16)

            load_x(0, 0, 0)
            sp.dma_start(raw2[0], wkv_in[0]).then_inc(s_raw[0], 16)
            sp.dma_start(raw2[1], wkv_in[1]).then_inc(s_raw[1], 16)
            load_x(1, 1, 1)
            sp.dma_start(bkv, bkv_in.to_broadcast((P, 2 * HID))).then_inc(s_bias, 16)
            for k in (2, 3):
                sp.wait_ge(s_wlo, k - 1)
                sp.dma_start(raw2[k % 2], wkv_in[k]).then_inc(s_raw[k % 2], 16)
            sp.dma_start(wg[:, :, :], wg_in.rearrange("(k p) n -> p k n", p=P)).then_inc(s_wg, 16)
            sp.wait_ge(s_trash, 1)
            sp.dma_start(lists.rearrange("(e p q) a -> p e (q a)", e=EXPERTS, p=P),
                         trash.rearrange("p (e q) -> p e q", e=EXPERTS)).then_inc(s_lists, 16)
            sp.wait_ge(s_lists, 16)
            sp.dma_start(bq[:, :], bq_in.to_broadcast((P, HEADS * HEAD_DIM))).then_inc(s_wg, 16)
            sp.wait_ge(s_zero, 1)
            for b in range((TOKENS + PAIR) // P):
                sp.dma_start(acc_dram[b * P:(b + 1) * P, :], zero).then_inc(s_zeroed, 16)
            for b in range(TOKENS // P, (TOKENS + PAIR) // P):
                sp.dma_start(rows_dram[b * P:(b + 1) * P, 0:HID], zero).then_inc(s_zeroed, 16)
                sp.dma_start(rows_dram[b * P:(b + 1) * P, HID:ROW], zero[:, 0:EXPERTS]).then_inc(s_zeroed, 16)

            def a_body(u, s):
                if not (isinstance(u, int) and u + 2 > 31):
                    load_x(u + 2, s, u + 2)
                if isinstance(u, int) and u < 16:
                    return
                if s_wq_on[0]:
                    wait(sp, s_wlo, KC + u - 17)
                    sp.dma_start(raw2[s][:, 0:HID], wq_in[bass.ds(u - 16, 1), :, :].rearrange("a p n -> p (a n)")
                                 ).then_inc(s_raw[s], 16)

            s_wq_on = [False]
            a_body(0, 0)
            a_body(1, 1)
            pairs_of(2, 16, sp, a_body)
            s_wq_on[0] = True
            a_body(16, 0)
            a_body(17, 1)
            pairs_of(18, 30, sp, a_body)
            a_body(30, 0)
            a_body(31, 1)
            load_x(TILES, 0, 0)
            load_x(TILES + 1, 1, 1)

            def load_wo(b):
                for c in range(HEADS // 2):
                    if b == 0 and c < 2:
                        sp.wait_ge(s_wlo, KC + 15 + c)
                    else:
                        sp.wait_ge(s_m, HEADS * b + 2 * c - 2)
                    sp.dma_start(raw2[c % 2].rearrange("p (a n) -> p a n", a=2),
                                 wo_in[2 * c:2 * c + 2, :, :].rearrange("a p n -> p a n")).then_inc(s_raw[c % 2], 16)

            def b_body(t, s, b):
                if live(t, 2):
                    sp.wait_ge(s_x2, t - 1)
                    sp.dma_start(x2_dram[bass.ds((t - 2) * P, P), :], XRES[:, s, :]).then_inc(s_x2st[s], 16)
                if live(t, 3):
                    sp.wait_ge(s_wd, t - 2)
                    sp.dma_start(rows_dram[bass.ds((t - 3) * P, P), :], row[:, 1 - s, :]).then_inc(s_rst[1 - s], 16)
                if isinstance(t, int) and t + 2 < TILES or not isinstance(t, int):
                    load_x(t + TILES + 2, s, t + 2)
                if live(t):
                    if not (isinstance(t, int) and t < 2):
                        sp.wait_ge(s_x2st[s], (t - s) * 8)
                        sp.wait_ge(s_row, t - 1)
                    sp.dma_start(XRES[:, s, :], x_in[bass.ds(t * P, P), :]).then_inc(s_xres[s], 16)

            b_body(0, 0, 0)
            load_wo(0)
            for t in (1, 2, 3):
                b_body(t, t % 2, 0)
            pairs_of(4, 16, sp, lambda t, s: b_body(t, s, 0))
            b_body(16, 0, 1)
            load_wo(1)
            b_body(17, 1, 1)
            pairs_of(18, 30, sp, lambda t, s: b_body(t, s, 1))
            for t in range(30, 35):
                b_body(t, t % 2, 1)
            moe_sp(sp)

        @block.tensor
        def _(pe):
            def split_matmuls(ps, terms, start=True, stop=True, inc=None):
                for i, (w, m) in enumerate(terms):
                    last = nc.tensor.matmul(ps, w, m, start=start and i == 0, stop=stop and i == len(terms) - 1)
                return last

            def three(wh, wl, mh, ml):
                return [(wl, mh), (wh, ml), (wh, mh)]

            def t_x(u, s, du=1):
                pe.wait_ge(s_xn, u + 1)
                wait(pe, s_xl, u)
                if isinstance(u, int) and u in (TILES + 2, TILES + BATCH_TILES + 2):
                    pe.wait_ge(s_ktc, 1 + (u - TILES) // BATCH_TILES)
                for k in range(KC):
                    last = nc.tensor.transpose(pt[:, k * P:(k + 1) * P], XN[:, k * P:(k + 1) * P], ident[:, :])
                last.then_inc(s_xt, 1)

            def kv_tile(u, s):
                wait(pe, s_z, u - 1)
                pe.wait_ge(s_xl, u + 1)
                for c, (ps, done) in enumerate(((pk[s], s_k), (pv[s], s_v))):
                    terms = []
                    for k in range(KC):
                        cols = slice(k * 2 * HID + c * HID, k * 2 * HID + (c + 1) * HID)
                        terms += three(XH[:, s, k, :], XL[:, s, k, :], wkv_hi[:, cols], wkv_lo[:, cols])
                    if c:
                        wait(pe, s_vx, u - 1)
                    split_matmuls(ps[:, :], terms).then_inc(done, 1)

            def kv_clear(b):
                wait(pe, s_kvev, b)
                for i in range(2):
                    nc.tensor.matmul(pkv[i][:, :], zero[:, 0:P], zero, start=True, stop=False, skip_group_check=True)

            def kv_add(u, s, stop=False):
                pe.wait_ge(s_sk, u + 1)
                pe.wait_ge(s_vx, u + 1)
                n = HEAD_DIM + 1
                for h in range(KV_HEADS):
                    last = nc.tensor.matmul(pkv[h // 2][:, (h % 2) * 256:(h % 2) * 256 + n], sk[:, s, h * P:(h + 1) * P],
                                            vx[:, s, h, 0:n], start=False, stop=stop, skip_group_check=True)
                last.then_inc(s_acc, 1)

            def a_body(u, s):
                t_x(u + 1, 1 - s)
                kv_tile(u, s)
                if isinstance(u, int) and u == 0:
                    return
                if isinstance(u, int) and u in (1, 17):
                    kv_clear(u // 16)
                kv_add(u - 1, 1 - s, stop=isinstance(u, int) and u == 16)

            pe.wait_ge(s_const, 1)
            pe.wait_ge(s_consts2, 4)
            pe.wait_ge(s_zero, 1)
            t_x(0, 0)
            pe.wait_ge(s_wlo, KC)
            run_a(pe, a_body)
            kv_add(TILES - 1, 1, stop=True)

            for b in range(BATCH):
                pe.wait_ge(s_diag, KV_HEADS * (b + 1))
                wait(pe, s_ksum, b)
                nc.tensor.matmul(pr[:, :], ones[:, :], prod, start=True, stop=True).then_inc(s_ksb, 1)

            pe.wait_ge(s_wlo, KC + 16)
            pe.wait_ge(s_wg, 32)

            def fold(b):
                pe.wait_ge(s_xl, TILES + BATCH_TILES * b + 2)
                for h in range(KV_HEADS):
                    last = nc.tensor.transpose(pt[:, h * P:(h + 1) * P], kvs[b][:, h, 0:HEAD_DIM], ident[:, :])
                last.then_inc(s_kt, 1)
                pe.wait_ge(s_ktc, b + 1)
                pe.wait_ge(s_zq, 64 * b + 4)
                for h in range(HEADS):
                    if h >= 2:
                        pe.wait_ge(s_mlo, HEADS * b + h - 1)
                    if h % 2 == 0:
                        base = (KC // 2 + 8 + 4 * b) * 16
                        pe.wait_ge(s_raw[h // 2 % 2], base + 16 * (h // 4 + 1))
                    nc.tensor.matmul(pq[h % 2][:, :], kvt[:, h // GROUP, :], raw2[h // 2 % 2][:, (h % 2) * HID:(h % 2 + 1) * HID],
                                     start=True, stop=True).then_inc(s_m, 1)
                pe.wait_ge(s_mlo, HEADS * (b + 1))

            def b_body(t, s, b):
                fixed = isinstance(t, int)
                for c in range(CHUNKS):
                    j = 4 * t + c
                    if live(t):
                        if c == 0:
                            pe.wait_ge(s_xl, t + TILES + 1)
                        wait(pe, s_zq, j - 1)
                        terms = []
                        for k in range(KC):
                            cols = slice(k * HEADS * P + c * HID, k * HEADS * P + (c + 1) * HID)
                            terms += three(XH[:, s, k, :], XL[:, s, k, :], wq_hi[:, cols], wq_lo[:, cols])
                        split_matmuls(pq[c % 2][:, :], terms).then_inc(s_q, 1)
                    if not fixed or 0 <= j - 2 < 4 * TILES:
                        i = (c - 2) % 2
                        pe.wait_ge(s_scale, j - 1)
                        wait(pe, s_slo, j - 3)
                        for h in range(GROUP):
                            last = nc.tensor.transpose(pst[i][:, h * P:(h + 1) * P], sqn[:, i, h * P:(h + 1) * P], ident[:, :])
                        last.then_inc(s_st, 1)
                    if c == 2 and live(t, 2):
                        pe.wait_ge(s_row, t - 1)
                        wait(pe, s_rk, 2 * t - 4)
                        for k in range(KC):
                            last = nc.tensor.transpose(pr[:, k * P:(k + 1) * P], row[:, s, k * P:(k + 1) * P], ident[:, :])
                        last.then_inc(s_rt, 1)
                    if c == 3 and live(t, 2):
                        pe.wait_ge(s_x2t, t - 1)
                        for k in range(KC):
                            last = nc.tensor.matmul(pr[:, 0:EXPERTS], x2t[:, k, :], wg[:, k, :], start=k == 0, stop=k == KC - 1)
                        last.then_inc(s_lgt, 1)
                    if fixed and c == 3 and t in (0, BATCH_TILES):
                        fold(b)
                    if not fixed or 0 <= j - 3 < 4 * TILES:
                        i, cc = (c - 3) % 2, (c - 3) % 4
                        tile_parity = s if c == 3 else 1 - s
                        ot = t if c == 3 else t - 1
                        pe.wait_ge(s_slo, j - 2)
                        if cc == 0:
                            wait(pe, s_on, ot - 1)
                        terms = []
                        for h in range(GROUP):
                            cols = slice((cc * GROUP + h) * HID, (cc * GROUP + h + 1) * HID)
                            terms += three(SH[:, i, h, :], SL[:, i, h, :], m_hi[:, cols], m_lo[:, cols])
                        split_matmuls(po[tile_parity][:, :], terms, start=cc == 0, stop=cc == 3).then_inc(s_o, 1)
                    if c == 0 and live(t, 3):
                        pe.wait_ge(s_msk, t - 2)
                        pe.wait_ge(s_lg, t - 2)
                        nc.tensor.matmul(pr[:, 64:64 + EXPERTS], upper[:, :], msk[:, :], start=True, stop=True)
                        nc.tensor.matmul(pr[:, 128:128 + EXPERTS], ones[:, :], msk[:, :], start=True,
                                         stop=True).then_inc(s_rank, 1)
                    if c == 2 and (not fixed or t + 1 < TILES):
                        t_x(t + TILES + 1, 1 - s)

            run_b(pe, b_body)
            moe_pe(pe)

        @block.scalar
        def _(act):
            def x_high(u, s, free, at_least):
                act.wait_ge(s_xt, u + 1)
                wait(act, free, at_least)
                nc.scalar.activation(XH[:, s, :, :].rearrange("p k n -> p (k n)"), pt[:, :], ACT.Copy).then_inc(s_xh, 1)

            def w_high(dst, src, sem_loaded, value):
                act.wait_ge(sem_loaded, value)
                nc.scalar.activation(dst, src, ACT.Copy).then_inc(s_whi, 1)

            for k in range(KC):
                w_high(wkv_hi[:, k * 1024:(k + 1) * 1024], raw2[k % 2], s_raw[k % 2], 16 * (k // 2 + 1))
            x_high(0, 0, s_v, 0)

            def a_body(u, s):
                x_high(u + 1, 1 - s, s_v, u)
                act.wait_ge(s_z, u + 1)
                wait(act, s_sk, u)
                nc.scalar.activation(ek, zk, ACT.Relu, scale=-1.0).then_inc(s_nr, 1)
                act.wait_ge(s_nr, u + 1)
                nc.scalar.activation(ek, ek, ACT.Exp, scale=-1.0).then_inc(s_e, 1)
                if isinstance(u, int) and u == 16:
                    kv_out(0)
                if not isinstance(u, int) and not second[0]:
                    return
                if isinstance(u, int) and u < 16:
                    return
                w_high(wq_hi[:, bass.ds((u - 16) * HID, HID)], raw2[s][:, 0:HID], s_raw[s], 16 * (KC // 2) + (u - 16 - s) * 8 + 16)

            def kv_out(b):
                act.wait_ge(s_acc, BATCH_TILES * (b + 1))
                for i in range(2):
                    last = nc.scalar.activation(kvs[b][:, 2 * i:2 * i + 2, :],
                                                pkv[i][:, :].rearrange("p (h n) -> p h n", h=2)[:, :, 0:HEAD_DIM + 1], ACT.Copy)
                last.then_inc(s_kvev, 1)

            second = [False]
            a_body(0, 0)
            a_body(1, 1)
            pairs_of(2, 16, act, a_body)
            second[0] = True
            a_body(16, 0)
            a_body(17, 1)
            pairs_of(18, 32, act, a_body)
            kv_out(1)

            def fold(b):
                act.wait_ge(s_kt, b + 1)
                nc.scalar.activation(kvt[:, :, :].rearrange("p h n -> p (h n)"), pt[:, :], ACT.Copy).then_inc(s_ktc, 1)
                for h in range(HEADS):
                    act.wait_ge(s_m, HEADS * b + h + 1)
                    nc.scalar.activation(m_hi[:, h * HID:(h + 1) * HID], pq[h % 2][:, :], ACT.Copy).then_inc(s_mhi, 1)

            def b_body(t, s, b):
                fixed = isinstance(t, int)
                for c in range(CHUNKS):
                    j = 4 * t + c
                    if not fixed or 0 <= j - 2 < 4 * TILES:
                        i = (c - 2) % 2
                        act.wait_ge(s_st, j - 1)
                        wait(act, s_o, j - 3)
                        nc.scalar.activation(SH[:, i, :, :].rearrange("p h n -> p (h n)"), pst[i][:, :],
                                             ACT.Copy).then_inc(s_shi, 1)
                    if c == 3 and (not fixed or t + 1 < TILES):
                        x_high(t + TILES + 1, 1 - s, s_q, 4 * t) if not (fixed and t == 0) else x_high(TILES + 1, 1, s_v, TILES)
                    if fixed and c == 3 and t in (0, BATCH_TILES):
                        fold(b)
                    if live(t):
                        act.wait_ge(s_zq, j + 1)
                        wait(act, s_sq, j - 1)
                        nc.scalar.activation(e[:, c % 2, :], z[:, c % 2, :], ACT.Relu, scale=-1.0).then_inc(s_nq, 1)
                        act.wait_ge(s_nq, j + 1)
                        nc.scalar.activation(e[:, c % 2, :], e[:, c % 2, :], ACT.Exp, scale=-1.0).then_inc(s_eq, 1)
                    if c == 2 and live(t, 2):
                        act.wait_ge(s_rt, t - 1)
                        wait(act, s_lgt, t - 2)
                        nc.scalar.activation(x2t[:, :, :].rearrange("p k n -> p (k n)"), pr[:, :], ACT.Copy).then_inc(s_x2t, 1)
                    if c == 3 and live(t, 1):
                        act.wait_ge(s_nmr, t)
                        wait(act, s_x2, t - 1)
                        nc.scalar.activation(on, po[1 - s][:, :], ACT.Identity, bias=nmr[:, 0:1], scale=rs[:, 1:2]).then_inc(s_on, 1)
                    if c == 3 and live(t, 2):
                        act.wait_ge(s_nmx, t - 1)
                        wait(act, s_wun, t - 2)
                        nc.scalar.activation(ex[:, :], lg[:, :], ACT.Exp, bias=negmax[:, 0:1]).then_inc(s_ex, 1)

            act.wait_ge(s_zeroed, 16 * (TOKENS // P + 3 * PAIR // P))
            run_b(act, b_body)
            moe_act(act)

        @block.vector
        def _(dve):
            nc.vector.memset(ones[:, :], 1.0)
            nc.vector.memset(zero, 0.0).then_inc(s_zero, 1)
            nc.vector.memset(vx[:, :, :, HEAD_DIM:HEAD_DIM + 2], 1.0)
            nc.vector.memset(mhalf2[:, :], -0.5)
            nc.vector.memset(mhalf[:, :], -0.5).then_inc(s_const, 1)

            def mean_var(src, slot, s_stats, s_out, n):
                nc.vector.bn_stats(bst[:, slot, :], src).then_inc(s_stats, 1)
                dve.wait_ge(s_stats, n)
                stand(dve)
                nc.vector.bn_aggr(mv[:, slot, :], bst[:, slot, :]).then_inc(s_out, 1)

            def x_stats(u, s, loads):
                dve.wait_ge(s_x[s], 16 * loads)
                mean_var(X[:, s, :], 0, s_bs, s_mv, u + 1)

            def x_norm(u, s):
                dve.wait_ge(s_rs, u + 1)
                wait(dve, s_xt, u)
                nc.vector.tensor_scalar(XN[:, :], X[:, s, :], mv[:, 0, 0:1], rs[:, 0:1], ALU.subtract, ALU.mult).then_inc(s_xn, 1)

            def x_low(u, s):
                dve.wait_ge(s_xh, u + 1)
                hi = XH[:, s, :, :].rearrange("p k n -> p (k n)")
                nc.vector.tensor_tensor(XL[:, s, :, :].rearrange("p k n -> p (k n)"), pt[:, :], hi.bitcast(f32),
                                        ALU.subtract).then_inc(s_xl, 1)

            def w_low(lo, hi, src, n):
                dve.wait_ge(s_whi, n)
                nc.vector.tensor_tensor(lo, src, hi.bitcast(f32), ALU.subtract).then_inc(s_wlo, 1)

            x_stats(0, 0, 1)
            x_norm(0, 0)
            for k in range(KC):
                w_low(wkv_lo[:, k * 1024:(k + 1) * 1024], wkv_hi[:, k * 1024:(k + 1) * 1024], raw2[k % 2], k + 1)
            x_low(0, 0)
            x_stats(1, 1, 1)
            x_norm(1, 1)
            dve.wait_ge(s_bias, 16)

            def a_body(u, s):
                dve.wait_ge(s_k, u + 1)
                nc.vector.tensor_tensor(zk, pk[s][:, :], bkv[:, 0:HID], ALU.add).then_inc(s_z, 1)
                more = not (isinstance(u, int) and u == TILES - 1)
                if more:
                    dve.wait_ge(s_x[s], (u - s) * 8 + 32)
                    mean_var(X[:, s, :], 0, s_bs, s_mv, u + 3)
                x_low(u + 1, 1 - s)
                dve.wait_ge(s_v, u + 1)
                wait(dve, s_acc, u - 1)
                nc.vector.tensor_tensor(vx[:, s, :, 0:HEAD_DIM], pv[s][:, :].rearrange("p (h n) -> p h n", h=KV_HEADS),
                                        bkv[:, HID:2 * HID].rearrange("p (h n) -> p h n", h=KV_HEADS), ALU.add).then_inc(s_vx, 1)
                dve.wait_ge(s_e, u + 1)
                nc.vector.scalar_tensor_tensor(sk[:, s, :], zk, 1.0, ek, ALU.add, ALU.max).then_inc(s_sk, 1)
                if more:
                    x_norm(u + 2, s)
                if (isinstance(u, int) and u < 16) or not second[0]:
                    return
                cols = bass.ds((u - 16) * HID, HID)
                w_low(wq_lo[:, cols], wq_hi[:, cols], raw2[s][:, 0:HID], KC + u - 15)

            second = [False]
            a_body(0, 0)
            a_body(1, 1)
            pairs_of(2, 16, dve, a_body)
            second[0] = True
            a_body(16, 0)
            a_body(17, 1)
            pairs_of(18, 30, dve, a_body)
            a_body(30, 0)
            a_body(31, 1)

            dve.wait_ge(s_consts2, 7)
            for b in range(BATCH):
                dve.wait_ge(s_kvev, BATCH)
                wait(dve, s_ksb, b)
                for h in range(KV_HEADS):
                    nc.vector.tensor_scalar(prod[:, h * P:(h + 1) * P], ident[:, :], kvs[b][:, h, HEAD_DIM:HEAD_DIM + 1], None,
                                            ALU.mult).then_inc(s_diag, 1)
                dve.wait_ge(s_ksb, b + 1)
                nc.vector.tensor_copy(ksumb[b][:, :], pr[:, :]).then_inc(s_ksum, 1)

            dve.wait_ge(s_wg, 32)

            def fold(b):
                for h in range(HEADS):
                    dve.wait_ge(s_mhi, HEADS * b + h + 1)
                    cols = slice(h * HID, (h + 1) * HID)
                    nc.vector.tensor_tensor(m_lo[:, cols], pq[h % 2][:, :], m_hi[:, cols].bitcast(f32), ALU.subtract).then_inc(s_mlo, 1)

            def norm_rec(j, i):
                dve.wait_ge(s_prod, j + 1)
                nc.vector.tensor_reduce(nrm[:, :], prod.rearrange("p (h n) -> p h n", h=GROUP), AX.X, ALU.add).then_inc(s_red, 1)
                dve.wait_ge(s_red, j + 1)
                nc.vector.tensor_scalar(nre[:, :], nrm[:, :], ATTN_EPS, None, ALU.add).then_inc(s_eps, 1)
                dve.wait_ge(s_eps, j + 1)
                nc.vector.reciprocal(rec[:, i, :], nre[:, :]).then_inc(s_rec, 1)

            def route(t):
                dve.wait_ge(s_lgt, t + 1)
                wait(dve, s_ex, t)
                nc.vector.tensor_copy(lg[:, :], pr[:, 0:EXPERTS]).then_inc(s_lg, 1)
                dve.wait_ge(s_lg, t + 1)
                stand(dve)
                nc.vector.max(mx8[:, :], lg[:, :]).then_inc(s_mx, 1)
                dve.wait_ge(s_mx, t + 1)
                nc.vector.tensor_scalar(negmax[:, :], mx8[:, 0:1], -1.0, None, ALU.mult).then_inc(s_nmx, 1)
                nc.vector.max_index(ix8[:, :], mx8[:, :], lg[:, :]).then_inc(s_ix, 1)
                dve.wait_ge(s_ix, t + 1)
                wait(dve, s_ri, 2 * t)
                nc.vector.tensor_copy(ixf[:, :], ix8[:, :]).then_inc(s_ixf, 1)
                dve.wait_ge(s_ixf, t + 1)
                wait(dve, s_posf, t)
                nc.vector.tensor_tensor(oh[:, :, :], ixf[:, :].rearrange("p (k a) -> p k a", a=1).to_broadcast((P, TOP_K, EXPERTS)),
                                        iota_e[:, :].rearrange("p (a n) -> p a n", a=1).to_broadcast((P, TOP_K, EXPERTS)),
                                        ALU.is_equal).then_inc(s_oh, 1)
                dve.wait_ge(s_oh, t + 1)
                wait(dve, s_rank, t)
                wait(dve, s_wun, t)
                nc.vector.tensor_reduce(msk[:, :], oh[:, :, :].rearrange("p k n -> p n k"), AX.X, ALU.add).then_inc(s_msk, 1)

            def place(t, s):
                dve.wait_ge(s_ex, t + 1)
                dve.wait_ge(s_msk, t + 1)
                nc.vector.tensor_tensor(wun[:, :], ex[:, :], msk[:, :], ALU.mult).then_inc(s_wun, 1)
                dve.wait_ge(s_wun, t + 1)
                nc.vector.reduce_sum(wsum[:, :], wun[:, :], AX.X).then_inc(s_wsum, 1)
                dve.wait_ge(s_rank, t + 1)
                wait(dve, s_rk, 2 * t)
                nc.vector.tensor_tensor(rank[:, :], pr[:, 64:64 + EXPERTS], carry[:, :], ALU.add).then_inc(s_rk, 1)
                dve.wait_ge(s_wsum, t + 1)
                nc.vector.reciprocal(wrec[:, :], wsum[:, :]).then_inc(s_wrec, 1)
                dve.wait_ge(s_rk, 2 * t + 1)
                nc.vector.tensor_tensor(carry[:, :], pr[:, 128:128 + EXPERTS], carry[:, :], ALU.add).then_inc(s_rk, 1)
                nc.vector.tensor_tensor(oh[:, :, :], oh[:, :, :],
                                        rank[:, :].rearrange("p (a n) -> p a n", a=1).to_broadcast((P, TOP_K, EXPERTS)),
                                        ALU.mult).then_inc(s_pf, 1)
                dve.wait_ge(s_wrec, t + 1)
                nc.vector.tensor_scalar(row[:, s, W_COL:W_COL + EXPERTS], wun[:, :], wrec[:, 0:1], None, ALU.mult).then_inc(s_wd, 1)
                dve.wait_ge(s_pf, t + 1)
                nc.vector.reduce_sum(posf[:, :], oh[:, :, :], AX.X).then_inc(s_posf, 1)
                wait(dve, s_id, 2 * t)
                wait(dve, s_sc[s], (t - s) * 64)
                nc.vector.tensor_copy(ids[:, s, :], idf[:, :]).then_inc(s_id, 1)
                dve.wait_ge(s_id, 2 * t + 1)
                nc.vector.tensor_scalar(idf[:, :], idf[:, :], float(P), None, ALU.add).then_inc(s_id, 1)
                dve.wait_ge(s_posf, t + 1)
                nc.vector.tensor_copy(rank_i[:, :], posf[:, :]).then_inc(s_ri, 1)
                nc.vector.tensor_scalar(at_f[:, :], ixf[:, :], float(CAP), None, ALU.mult).then_inc(s_ri, 1)
                dve.wait_ge(s_ri, 2 * t + 2)
                nc.vector.tensor_scalar(col_i[:, :], rank_i[:, :], P.bit_length() - 1, None, ALU.arith_shift_right).then_inc(s_ci, 1)
                nc.vector.scalar_tensor_tensor(at_f[:, :], posf[:, :], float(COLS), at_f[:, :], ALU.mult, ALU.add).then_inc(s_ci, 1)
                dve.wait_ge(s_ci, 2 * t + 2)
                nc.vector.tensor_copy(col_f[:, :], col_i[:, :]).then_inc(s_cf, 1)
                dve.wait_ge(s_cf, t + 1)
                nc.vector.scalar_tensor_tensor(pos[:, s, :], col_f[:, :], float(1 - P * COLS), at_f[:, :], ALU.mult, ALU.add).then_inc(s_pos, 1)

            def b_body(t, s, b):
                fixed = isinstance(t, int)
                for c in range(CHUNKS):
                    j = 4 * t + c
                    i = c % 2
                    if live(t):
                        dve.wait_ge(s_q, j + 1)
                        nc.vector.tensor_tensor(z[:, i, :], pq[i][:, :], bq[:, c * HID:(c + 1) * HID], ALU.add).then_inc(s_zq, 1)
                    if not fixed or 0 <= j - 2 < 4 * TILES:
                        dve.wait_ge(s_shi, j - 1)
                        nc.vector.tensor_tensor(SL[:, i, :, :].rearrange("p h n -> p (h n)"), pst[i][:, :],
                                                SH[:, i, :, :].rearrange("p h n -> p (h n)").bitcast(f32), ALU.subtract).then_inc(s_slo, 1)
                    if not fixed or 0 <= j - 1 < 4 * TILES:
                        norm_rec(j - 1, 1 - i)
                    if c == 0 and live(t, 2):
                        dve.wait_ge(s_on, t - 1)
                        dve.wait_ge(s_xres[s], (t - 2 - s) * 8 + 16)
                        nc.vector.tensor_tensor(XRES[:, s, :], XRES[:, s, :], on, ALU.add).then_inc(s_x2, 1)
                        dve.wait_ge(s_x2, t - 1)
                        mean_var(XRES[:, s, :], 2, s_2bs, s_2mv, t - 1)
                    if c == 0 and (not fixed or t + 1 < TILES):
                        dve.wait_ge(s_x[1 - s], 16 * (TILES // 2) + (t + 1 - (1 - s)) * 8 + 16)
                        mean_var(X[:, 1 - s, :], 0, s_bs, s_mv, t + TILES + 2)
                    if c == 1 and live(t, 3):
                        place(t - 3, 1 - s)
                    if c == 1 and live(t, 2):
                        dve.wait_ge(s_2rs, t - 1)
                        wait(dve, s_rst[s], (t - 2 - s) * 8)
                        nc.vector.tensor_scalar(row[:, s, 0:HID], XRES[:, s, :], mv[:, 2, 0:1], rs[:, 2:3], ALU.subtract,
                                                ALU.mult).then_inc(s_row, 1)
                    if c == 1 and (not fixed or t + 1 < TILES):
                        x_norm(t + TILES + 1, 1 - s)
                    if c == 3 and (not fixed or t + 1 < TILES):
                        x_low(t + TILES + 1, 1 - s)
                    if fixed and c == 3 and t in (0, BATCH_TILES):
                        fold(b)
                    if c == 3 and live(t, 1):
                        dve.wait_ge(s_o, 4 * t)
                        mean_var(po[1 - s][:, :], 1, s_obs, s_omv, t)
                    if c == 3 and live(t, 2):
                        route(t - 2)
                    if live(t):
                        dve.wait_ge(s_eq, j + 1)
                        wait(dve, s_scale, j - 1)
                        nc.vector.scalar_tensor_tensor(sq[:, i, :], z[:, i, :], 1.0, e[:, i, :], ALU.add, ALU.max).then_inc(s_sq, 1)
                    if c == 3 and live(t, 1):
                        dve.wait_ge(s_ors, t)
                        nc.vector.tensor_scalar(nmr[:, :], mv[:, 1, 0:1], -1.0, rs[:, 1:2], ALU.mult, ALU.mult).then_inc(s_nmr, 1)

            run_b(dve, b_body)
            moe_dve(dve)

        @block.gpsimd
        def _(pool):
            nc.gpsimd.memset(ident[:, :], 0.0).then_inc(s_consts2, 1)
            nc.gpsimd.memset(upper[:, :], 1.0).then_inc(s_consts2, 1)
            pool.wait_ge(s_consts2, 2)
            nc.gpsimd.affine_select(out=ident[:, :], in_=ident[:, :], compare_op=ALU.not_equal, fill=1.0, base=0,
                                    pattern=[[-1, P]], channel_multiplier=1).then_inc(s_consts2, 1)
            nc.gpsimd.affine_select(out=upper[:, :], in_=upper[:, :], compare_op=ALU.is_gt, fill=0.0, base=0,
                                    pattern=[[1, P]], channel_multiplier=-1).then_inc(s_consts2, 1)

            def rstd(slot, s_in, s_mid, s_out, n):
                pool.wait_ge(s_in, n)
                stand(pool)
                nc.gpsimd.tensor_scalar(ve[:, slot:slot + 1], mv[:, slot, 1:2], NORM_EPS, None, ALU.add).then_inc(s_mid, 1)
                pool.wait_ge(s_mid, n)
                nc.gpsimd.tensor_tensor(rs[:, slot:slot + 1], ve[:, slot:slot + 1], mhalf[:, :], ALU.pow).then_inc(s_out, 1)

            nc.gpsimd.iota(trash, [[0, EXPERTS], [0, COLS // 2], [P, 2]], base=TRASH, channel_multiplier=1).then_inc(s_trash, 1)
            pool.wait_ge(s_const, 1)
            rstd(0, s_mv, s_ve, s_rs, 1)
            nc.gpsimd.iota(iota_e[:, :], [[1, EXPERTS]], base=0, channel_multiplier=0, allow_small_or_imprecise_dtypes=True).then_inc(s_consts2, 1)
            nc.gpsimd.iota(carry[:, :], [[0, EXPERTS]], base=0, channel_multiplier=0, allow_small_or_imprecise_dtypes=True).then_inc(s_consts2, 1)
            nc.gpsimd.iota(idf[:, :], [[0, 1]], base=0, channel_multiplier=1, allow_small_or_imprecise_dtypes=True).then_inc(s_consts2, 1)
            rstd(0, s_mv, s_ve, s_rs, 2)
            with pool.Fori(2, TILES + 1) as u:
                rstd(0, s_mv, s_ve, s_rs, u + 1)

            pool.wait_ge(s_ksum, 2)
            pool.wait_ge(s_lists, 16)
            def send(t, s, k0, k1):
                if k0 == 0:
                    pool.wait_ge(s_pos, t + 1)
                    pool.wait_ge(s_id, 2 * t + 1)
                    stand(pool)
                for k in range(k0, k1):
                    nc.gpsimd.indirect_dma_start(lists[:, :], bass.IndirectOffsetOnAxis(pos[:, s, k:k + 1], 0), ids[:, s, :],
                                                 None).then_inc(s_sc[s], 16)

            def b_body(t, s, b):
                fixed = isinstance(t, int)
                for c in range(CHUNKS):
                    j = 4 * t + c
                    i = c % 2
                    if c == 0 and live(t, 4):
                        send(t - 4, s, 6, 8)
                    if not fixed or 0 <= j - 1 < 4 * TILES:
                        pool.wait_ge(s_rec, j)
                        wait(pool, s_st, j - 2)
                        nc.gpsimd.tensor_tensor(sqn[:, 1 - i, :].rearrange("p (h n) -> p h n", h=GROUP),
                                                sq[:, 1 - i, :].rearrange("p (h n) -> p h n", h=GROUP),
                                                rec[:, 1 - i, :].rearrange("p (h a) -> p h a", a=1).to_broadcast((P, GROUP, P)),
                                                ALU.mult).then_inc(s_scale, 1)
                    if c == 0 and live(t, 2):
                        rstd(2, s_2mv, s_2ve, s_2rs, t - 1)
                    if c == 0 and (not fixed or t + 1 < TILES):
                        rstd(0, s_mv, s_ve, s_rs, t + TILES + 2)
                    if c == 2 and live(t, 3):
                        send(t - 3, 1 - s, 0, 3)
                    if c == 3 and live(t, 3):
                        send(t - 3, 1 - s, 3, 6)
                    if c == 3 and live(t, 1):
                        rstd(1, s_omv, s_ove, s_ors, t)
                    if live(t):
                        pool.wait_ge(s_sq, j + 1)
                        wait(pool, s_red, j)
                        nc.gpsimd.tensor_tensor(prod.rearrange("p (h n) -> p h n", h=GROUP),
                                                sq[:, i, :].rearrange("p (h n) -> p h n", h=GROUP),
                                                ksumb[b][:, c * P:(c + 1) * P].rearrange("p (a n) -> p a n", a=1).to_broadcast((P, GROUP, P)),
                                                ALU.mult).then_inc(s_prod, 1)

            run_b(pool, b_body)
            moe_pool(pool)


def kernel(**inputs):
    import numpy as np
    import concourse.bacc as bacc
    from concourse.bass_utils import run_bass_kernel_spmd

    a = {k: np.asarray(v) for k, v in inputs.items()}
    w_kv = np.concatenate([a["L0_attn_Wk"], a["L0_attn_Wv"]], 0).T
    w_13 = np.concatenate([a["L0_ffn_w1"], a["L0_ffn_v1"]], 2)
    arrays = {
        "x_in": a["L0_attn_hidden_states"].reshape(TOKENS, HID),
        "wkv_in": w_kv.reshape(KC, P, 2 * HID),
        "bq_in": a["L0_attn_bq"].reshape(1, -1),
        "bkv_in": np.concatenate([a["L0_attn_bk"], a["L0_attn_bv"]]).reshape(1, -1),
        "wq_in": a["L0_attn_Wq"].T.reshape(KC, P, CHUNKS, HID).transpose(0, 2, 1, 3).reshape(KC * CHUNKS, P, HID),
        "wo_in": a["L0_attn_Wo"].T.reshape(HEADS, P, HID),
        "wg_in": a["L0_ffn_wg"].T,
        "w13_in": w_13.reshape(EXPERTS, KC, P, UP).transpose(0, 2, 1, 3).reshape(EXPERTS, P, W13),
        "w2_in": a["L0_ffn_w2"],
    }
    arrays = {k: np.ascontiguousarray(v) for k, v in arrays.items()}
    nc = bacc.Bacc("TRN2", target_bir_lowering=False, num_devices=1)
    args = [nc.dram_tensor(k, v.shape, mybir.dt.from_np(v.dtype), kind="ExternalInput").ap() for k, v in arrays.items()]
    out = nc.dram_tensor("out", (TOKENS, HID), mybir.dt.float32, kind="ExternalOutput").ap()
    x, wkv, bq, bkv, wq, wo, wg, w13, w2 = args
    layer(nc, x, wkv, bq, bkv, wq, wo, wg, w13, w2, out)
    got = run_bass_kernel_spmd(nc, [arrays], core_ids=[0]).results[0]["out"]
    return got.reshape(BATCH, SEQ, HID)
```

```python
import concourse.bass as bass
from concourse import mybir
from contextlib import ExitStack

BATCH, SEQ, HID = 2, 2048, 512
HEADS, KV_HEADS, HEAD_DIM = 16, 4, 128
EXPERTS, TOP_K, FFN = 32, 8, 192
P = 128
TOKENS = BATCH * SEQ
TILES = TOKENS // P
BATCH_TILES = SEQ // P
KC = HID // P
GROUP = HEADS // KV_HEADS
CHUNKS = HEADS // GROUP
ATTN_EPS, NORM_EPS = 1e-6, 1e-5

W_COL, ROW = HID, HID + EXPERTS
PAIR = 2 * P
CAP = TOKENS + PAIR
COLS = CAP // P
TRASH = TOKENS

UP = 2 * FFN
W13 = KC * UP
W2H, W2L, W2X = 2 * W13, 2 * W13 + HID, 2 * W13 + 2 * HID
WSET = 2 * W13 + 3 * HID
WSETS = 4
MAX_PAIRS = TOKENS * TOP_K // PAIR + 2 * EXPERTS
RING = 4
RAW_N = W13 + 2 * HID
FSTEPS = TOKENS // PAIR
PIECES = [(k * UP, UP) for k in range(KC)] + [(W13, HID), (W13 + HID, HID)]
FRING = 8
XRING = 14
FOUT = 4


def layer(nc, x_in, wkv_in, bq_in, bkv_in, wq_in, wo_in, wg_in, w13_in, w2_in, out):
    f32, f32r, i32, u32 = mybir.dt.float32, mybir.dt.float32r, mybir.dt.int32, mybir.dt.uint32
    ALU, ACT, AX = mybir.AluOpType, mybir.ActivationFunctionType, mybir.AxisListType

    lists = nc.dram_tensor("expert_lists", (EXPERTS * CAP, 1), i32, kind="Internal").ap()
    rows_dram = nc.dram_tensor("token_rows", (TOKENS + PAIR, ROW), f32, kind="Internal").ap()
    acc_dram = nc.dram_tensor("moe_sum", (TOKENS + PAIR, HID), f32, kind="Internal").ap()
    x2_dram = nc.dram_tensor("after_attention", (TOKENS, HID), f32, kind="Internal").ap()

    ctx = ExitStack()
    with ctx:
        def sb(name, shape, dt=f32):
            return ctx.enter_context(nc.sbuf_tensor(name, shape, dt))

        def sem(name):
            return ctx.enter_context(nc.semaphore(name))

        def wait(eng, s, v):
            if not (isinstance(v, int) and v <= 0):
                eng.wait_ge(s, v)

        def stand(eng):
            eng.sem_inc(s_stood, 1)

        WB = sb("WB", [P, 2 * KC * HEADS * HEAD_DIM + 2 * HEADS * HID], f32r)
        NQ, NM = KC * HEADS * HEAD_DIM, HEADS * HID
        wq_hi = WB[:, 0:NQ]
        wq_lo = WB[:, NQ:2 * NQ]
        m_hi = WB[:, 2 * NQ:2 * NQ + NM]
        m_lo = WB[:, 2 * NQ + NM:2 * NQ + 2 * NM]
        wkv_hi = m_hi[:, 0:KC * 2 * HID]
        wkv_lo = m_lo[:, 0:KC * 2 * HID]
        XH = sb("XH", [P, 2, KC, P], f32r)
        XL = sb("XL", [P, 2, KC, P], f32r)
        SH = sb("SH", [P, 2, GROUP, P], f32r)
        SL = sb("SL", [P, 2, GROUP, P], f32r)
        RAW = sb("RAW", [P, RAW_N])
        raw2 = [RAW[:, 1024 * i:1024 * (i + 1)] for i in range(2)]
        X = sb("X", [P, 2, HID])
        XN = sb("XN", [P, HID])
        XRES = sb("XRES", [P, 2, HID])
        BIG = sb("BIG", [P, 5120])
        bkv = BIG[:, 0:1024]
        zk = BIG[:, 1024:1536]
        ek = BIG[:, 1536:2048]
        sk = BIG[:, 2048:3072].rearrange("p (i n) -> p i n", i=2)
        vx = BIG[:, 3072:3072 + 2 * KV_HEADS * (HEAD_DIM + 2)].rearrange("p (i h n) -> p i h n", i=2, h=KV_HEADS)
        z = BIG[:, 0:1024].rearrange("p (i n) -> p i n", i=2)
        e = BIG[:, 1024:2048].rearrange("p (i n) -> p i n", i=2)
        sq = BIG[:, 2048:3072].rearrange("p (i n) -> p i n", i=2)
        sqn = BIG[:, 3072:4096].rearrange("p (i n) -> p i n", i=2)
        prod = BIG[:, 4096:4608]
        on = BIG[:, 4608:5120]
        xr = BIG[:, 0:2 * ROW].rearrange("p (i n) -> p i n", i=2)
        o = 2 * ROW
        sg = BIG[:, o:o + 2 * FFN].rearrange("p (i n) -> p i n", i=2)
        o += 2 * FFN
        hx = BIG[:, o:o + 2 * 2 * P].rearrange("p (i n) -> p i n", i=2)
        o += 4 * P
        wring = BIG[:, o:o + 2 * RING * EXPERTS].rearrange("p (i r n) -> p i r n", i=2, r=RING)
        yb = X
        bq = sb("bq", [P, HEADS * HEAD_DIM])
        row = sb("row", [P, 2, ROW])
        kvs0 = sb("kvs0", [P, KV_HEADS * (HEAD_DIM + 1)])
        kvs1 = sb("kvs1", [P, KV_HEADS * (HEAD_DIM + 1)])
        kvs = [t[:, :].rearrange("p (h n) -> p h n", h=KV_HEADS) for t in (kvs0, kvs1)]
        kvt = kvs0[:, 0:HID].rearrange("p (h n) -> p h n", h=KV_HEADS)
        x2t = kvt
        ksum1 = sb("ksum1", [P, HID])
        ksumb = [RAW[:, 2048:2048 + HID], ksum1]
        ident = sb("ident", [P, P])
        ones = sb("ones", [P, P])
        upper = sb("upper", [P, P])
        zero = on
        wg = sb("wg", [P, KC, EXPERTS])
        iota_e = sb("iota_e", [P, EXPERTS])
        carry = sb("carry", [P, EXPERTS])
        idf = sb("idf", [P, 1])
        bst = sb("bst", [P, 3, 6])
        mv = sb("mv", [P, 3, 2])
        ve = sb("ve", [P, 3])
        rs = sb("rs", [P, 3])
        mhalf = sb("mhalf", [P, 1])
        mhalf2 = sb("mhalf2", [P, 2])
        nmr = sb("nmr", [P, 3])
        nrm = sb("nrm", [P, GROUP])
        rec = sb("rec", [P, 2, GROUP])
        lg = sb("lg", [P, EXPERTS])
        mx8 = sb("mx8", [P, TOP_K])
        ix8 = sb("ix8", [P, TOP_K], u32)
        ixf = sb("ixf", [P, 2, TOP_K])
        negmax = sb("negmax", [P, 1])
        ex = sb("ex", [P, EXPERTS])
        oh = sb("oh", [P, TOP_K, EXPERTS])
        msk = sb("msk", [P, EXPERTS])
        wun = sb("wun", [P, EXPERTS])
        wsum = sb("wsum", [P, 1])
        wrec = sb("wrec", [P, 1])
        rank = sb("rank", [P, EXPERTS])
        posf = sb("posf", [P, TOP_K])
        pos = sb("pos", [P, 2, TOP_K], u32)
        cnt_f, cnt_i, pr_i, pr_f, inc_f = [oh[0:1, i, :] for i in range(5)]
        cnt_i, pr_i = cnt_i.bitcast(i32), pr_i.bitcast(i32)
        table = sb("table", [1, 2, EXPERTS], i32)
        rank_i = sb("rank_i", [P, TOP_K], i32)
        col_i = sb("col_i", [P, TOP_K], i32)
        col_f = sb("col_f", [P, TOP_K])
        at_f = sb("at_f", [P, TOP_K])
        ids = sb("ids", [P, 2, 1], i32)
        lst = sb("lst", [P, 2, COLS], i32)
        gidx = sb("gidx", [P, 2], i32)
        aidx = sb("aidx", [P, 2], i32)
        idring = sb("idring", [P, 2, RING], i32)
        trash = bq[:, 0:EXPERTS * COLS].bitcast(i32)

        fa, fx = [WB[:, at:at + n * 2 * HID].bitcast(f32).rearrange("p (r j n) -> p r j n", r=n, j=2)
                  for at, n in ((0, FRING), (WSETS * WSET, XRING))]
        fn = BIG[:, 0:4096].rearrange("p (r j n) -> p r j n", r=FOUT, j=2)
        n = FRING * 2
        fbs = XRES[:, 0, 0:6 * n].rearrange("p (r j n) -> p r j n", r=FRING, j=2)
        fmv = XRES[:, 0, 6 * n:8 * n].rearrange("p (r j n) -> p r j n", r=FRING, j=2)
        fve = XRES[:, 0, 8 * n:9 * n].rearrange("p (r j) -> p r j", r=FRING)
        frs = XRES[:, 0, 9 * n:10 * n].rearrange("p (r j) -> p r j", r=FRING)
        fnm = sb("fnm", [P, FRING, 2])

        bank = [ctx.enter_context(nc.psum_tensor(f"bank{i}", [P, HID], f32)) for i in range(8)]
        pt, pk, pv, pkv, pr = bank[0], bank[1:3], bank[3:5], bank[5:7], bank[7]
        pq, pst, po = bank[1:3], bank[3:5], bank[5:7]
        et, eu, eh, ed = [bank[0], bank[7]], bank[1:3], bank[3:5], bank[5:7]

        s_stood = sem("stood")
        s_const, s_consts2, s_bias, s_wg = sem("const"), sem("const_pool"), sem("bias_loaded"), sem("wg_loaded")
        s_zero, s_zeroed = sem("zero_ready"), sem("sum_zeroed")
        s_trash, s_lists = sem("padding_ids"), sem("lists_filled")
        s_raw = [sem("raw_loaded0"), sem("raw_loaded1")]
        s_whi, s_wlo = sem("weights_high"), sem("weights_low")
        s_x = [sem("x_loaded0"), sem("x_loaded1")]
        s_bs, s_mv, s_ve, s_rs, s_xn = sem("x_stats"), sem("x_meanvar"), sem("x_var_eps"), sem("x_rstd"), sem("x_norm")
        s_xt, s_xh, s_xl = sem("x_transposed"), sem("x_high"), sem("x_low")
        s_k, s_v, s_z, s_nr, s_e = sem("k_done"), sem("v_done"), sem("zk"), sem("zk_neg"), sem("zk_exp")
        s_sk, s_vx, s_acc, s_kvev = sem("sk"), sem("vx"), sem("kv_added"), sem("kv_evacuated")
        s_diag, s_ksb, s_ksum = sem("ksum_diag"), sem("ksum_spread"), sem("ksum_ready")
        s_q, s_zq, s_nq, s_eq, s_sq = sem("q_done"), sem("zq"), sem("zq_neg"), sem("zq_exp"), sem("sq")
        s_red, s_rec, s_scale = sem("norm_sum"), sem("norm_rec"), sem("scaled")
        s_st, s_shi, s_slo, s_o = sem("s_transposed"), sem("s_high"), sem("s_low"), sem("o_chunk")
        s_kt, s_ktc, s_m, s_mhi, s_mlo = sem("kv_transposed"), sem("kvt_copied"), sem("m_done"), sem("m_high"), sem("m_low")
        s_xres = [sem("xres_loaded0"), sem("xres_loaded1")]
        s_x2st = [sem("x2_stored0"), sem("x2_stored1")]
        s_obs, s_omv, s_ove, s_ors, s_on = sem("o_stats"), sem("o_meanvar"), sem("o_var_eps"), sem("o_rstd"), sem("o_norm")
        s_x2, s_2bs, s_2mv, s_2ve, s_2rs, s_row = (sem("x2"), sem("x2_stats"), sem("x2_meanvar"), sem("x2_var_eps"),
                                                   sem("x2_rstd"), sem("row"))
        s_rt, s_x2t, s_lgt, s_lg, s_mx, s_nmx, s_ix, s_ixf = (sem("x2_transposed"), sem("x2t"), sem("logits"), sem("lg"),
                                                              sem("mx8"), sem("negmax"), sem("ix8"), sem("ixf"))
        s_oh, s_msk, s_ex, s_rank, s_rk = sem("one_hot"), sem("mask"), sem("ex"), sem("rank_done"), sem("rank")
        s_wun, s_wsum, s_wrec, s_wd, s_pf, s_pos = (sem("w_raw"), sem("w_sum"), sem("w_rec"), sem("w_row"),
                                                    sem("pos_prod"), sem("pos"))
        s_posf, s_ri, s_ci, s_cf, s_id = sem("posf"), sem("rank_int"), sem("col_int"), sem("col_float"), sem("id_col")
        s_sc = [sem("ids_sent0"), sem("ids_sent1")]
        s_rst = [sem("row_stored0"), sem("row_stored1")]
        s_tab, s_tabd = sem("table_steps"), sem("table_ready")
        s_ewr, s_ehi, s_elo = sem("ew_loaded"), sem("ew_high"), sem("ew_low")
        s_pad, s_pad0 = sem("zero_pair_ready"), sem("padding_zeros")
        s_lst, s_lused = [sem("list_loaded0"), sem("list_loaded1")], sem("list_used")
        two = lambda name: [sem(f"{name}_{i}") for i in "AB"]
        s_ld = two("rows_loaded")
        s_T, s_exh, s_exl = two("e_transposed"), two("e_high"), two("e_low")
        s_U, s_sg, s_h = two("e_up"), two("e_silu"), two("e_act")
        s_H, s_hh, s_hl = two("e_act_transposed"), two("e_act_high"), two("e_act_low")
        s_D, s_y, s_add = two("e_down"), two("e_out"), two("e_added")
        s_wr = two("weights_in_ring")
        s_gi, s_ai = two("gather_index"), two("add_index")
        s_fl, s_fx = [sem(f"f_loaded{r}") for r in range(FRING)], sem("f_x2_loaded")
        s_fst = [sem(f"f_stored{r}") for r in range(FOUT)]
        s_fbs, s_fmv, s_fve, s_frs, s_fnm, s_fn, s_fo = (sem("f_stats"), sem("f_meanvar"), sem("f_var_eps"), sem("f_rstd"),
                                                         sem("f_shift"), sem("f_norm"), sem("f_out"))

        block = ctx.enter_context(nc.Block())

        def pairs_of(lo, hi, eng, body):
            with eng.Fori(lo // 2, hi // 2) as p:
                body(2 * p, 0)
                body(2 * p + 1, 1)

        A_PLAN = [(0, 2), (2, 16), (16, 18), (18, 32)]
        B_PLAN = [(0, 6), (6, 16), (16, 18), (18, 30), (30, 36)]

        def run_a(eng, body):
            for lo, hi in A_PLAN:
                if hi - lo > 6:
                    pairs_of(lo, hi, eng, body)
                else:
                    for u in range(lo, hi):
                        body(u, u % 2)

        def run_b(eng, body):
            for lo, hi in B_PLAN:
                if hi - lo > 7:
                    pairs_of(lo, hi, eng, lambda t, s, b=lo // BATCH_TILES: body(t, s, b))
                else:
                    for t in range(lo, hi):
                        body(t, t % 2, min(t // BATCH_TILES, 1))

        def live(t, lag=0):
            return not isinstance(t, int) or 0 <= t - lag < TILES

        def each_expert(eng, body):
            eng.wait_ge(s_tabd, 1)

            def one(e, q):
                n = eng.value_load(table[0:1, 0, bass.ds(e, 1)], min_val=2, max_val=TOKENS // PAIR)
                first = eng.value_load(table[0:1, 1, bass.ds(e, 1)], min_val=0, max_val=MAX_PAIRS)
                body(e, q, first, n)
                return first + n

            with eng.Fori(0, EXPERTS // WSETS - 1) as r:
                for q in range(WSETS):
                    one(r * WSETS + q, q)
            for e in range(EXPERTS - WSETS, EXPERTS):
                total = one(e, e % WSETS)
            return total

        def slot_of(g):
            return (g + RING) & (RING - 1)

        def moe_sp(sp):
            def load_weights(e):
                sp.dma_start(RAW[:, 0:W13], w13_in[bass.ds(e, 1), :, :].rearrange("a p n -> p (a n)")).then_inc(s_ewr, 16)
                sp.dma_start(RAW[:, W13:W13 + HID], w2_in[bass.ds(e, 1), 0:P, :].rearrange("a p n -> p (a n)")).then_inc(s_ewr, 16)
                for i in range(2):
                    sp.dma_start(RAW[i * 64:(i + 1) * 64, W13 + HID:RAW_N],
                                 w2_in[bass.ds(e, 1), P:FFN, :].rearrange("a p n -> p (a n)")).then_inc(s_ewr, 16)

            def load_list(e, i):
                sp.dma_start(lst[:, i, :], lists[bass.ds(e * CAP, CAP), :].rearrange("(p q) a -> p (q a)", p=P)).then_inc(s_lst[i], 16)

            sp.wait_ge(s_m, BATCH * HEADS)
            load_weights(0)
            sp.wait_ge(s_elo, 1)
            load_weights(1)
            for i in range(2):
                sp.wait_ge(s_sc[i], TILES // 2 * TOP_K * 16)
            load_list(0, 0)
            load_list(1, 1)

            def body(e, i):
                sp.wait_ge(s_lused, e + 1)
                stand(sp)
                load_list(e + 2, i)
                sp.wait_ge(s_elo, e + 2)
                stand(sp)
                load_weights(e + 2)

            sp.wait_ge(s_o, 4 * TILES)
            for i in range(2):
                sp.wait_ge(s_x2st[i], 16 * (TILES // 2))

            def load_x2(f, r):
                sp.dma_start(fx[:, bass.ds(r, 1), :, :].rearrange("p a j n -> p (a j) n"),
                             x2_dram[bass.ds(f * PAIR, PAIR), :].rearrange("(j p) n -> p j n", p=P)).then_inc(s_fx, 16)

            with sp.Fori(0, XRING) as r:
                body(2 * r, 0)
                load_x2(r, r)
                body(2 * r + 1, 1)
            for e in range(2 * XRING, EXPERTS - 2):
                body(e, e % 2)

            sp.wait_ge(s_tabd, 1)
            total = (sp.value_load(table[0:1, 1, EXPERTS - 1:EXPERTS], min_val=0, max_val=MAX_PAIRS)
                     + sp.value_load(table[0:1, 0, EXPERTS - 1:EXPERTS], min_val=2, max_val=TOKENS // PAIR))
            sp.wait_ge(s_T[0], total + 2)
            for i in range(2):
                sp.wait_ge(s_add[i], 16 * total + 64)
                stand(sp)

            def load(f, r):
                sp.dma_start(fa[:, r, :, :], acc_dram[bass.ds(f * PAIR, PAIR), :].rearrange("(j p) n -> p j n", p=P)).then_inc(s_fl[r], 16)

            def store(f, r):
                sp.wait_ge(s_fo, f + 1)
                sp.dma_start(out[bass.ds(f * PAIR, PAIR), :].rearrange("(j p) n -> p j n", p=P), fn[:, r, :, :]).then_inc(s_fst[r], 16)

            for f in range(FRING):
                load(f, f)

            for f in range(FSTEPS):
                store(f, f % FOUT)
                if f + FRING < FSTEPS:
                    load(f + FRING, f)
                if f + XRING < FSTEPS:
                    load_x2(f + XRING, f)
            for r in range(FOUT):
                sp.wait_ge(s_fst[r], 16 * (FSTEPS // FOUT))

        def moe_pe(pe):
            for s in range(2):
                for x in (s_T, s_U, s_D):
                    pe.sem_inc(x[s], 1)
                pe.sem_inc(s_H[s], 2 - s)

            def rows_t(g, s):
                pe.wait_ge(s_ld[s], 16 * g + 16)
                pe.wait_ge(s_exl[s], g + 1)
                for k in range(KC):
                    last = nc.tensor.transpose(et[s][:, k * P:(k + 1) * P], xr[:, s, k * P:(k + 1) * P], ident[:, :])
                last.then_inc(s_T[s], 1)

            def up(g, s, q):
                pe.wait_ge(s_exl[s], g + 2)
                pe.wait_ge(s_h[s], g + 1)
                w = WB[:, q * WSET:(q + 1) * WSET]
                for k in range(KC):
                    wh, wl = w[:, k * UP:(k + 1) * UP], w[:, W13 + k * UP:W13 + (k + 1) * UP]
                    nc.tensor.matmul(eu[s][:, 0:UP], XL[:, s, k, :], wh, start=k == 0, stop=False)
                    nc.tensor.matmul(eu[s][:, 0:UP], XH[:, s, k, :], wl, start=False, stop=False)
                    last = nc.tensor.matmul(eu[s][:, 0:UP], XH[:, s, k, :], wh, start=False, stop=k == KC - 1)
                last.then_inc(s_U[s], 1)

            def act_t(g, s):
                pe.wait_ge(s_h[s], g + 2)
                pe.wait_ge(s_hl[s], g + 2)
                for c in range(2):
                    last = nc.tensor.transpose(eh[s][:, c * P:(c + 1) * P], hx[:, s, c * P:(c + 1) * P], ident[:, :])
                last.then_inc(s_H[s], 1)

            def down(g, s, q):
                pe.wait_ge(s_hl[s], g + 3)
                pe.wait_ge(s_y[s], g + 3)
                w2h, w2l, w2x = [WB[:, q * WSET + o:q * WSET + o + HID] for o in (W2H, W2L, W2X)]
                nc.tensor.matmul(ed[s][:, :], SL[:, s, 0, :], w2h, start=True, stop=False)
                nc.tensor.matmul(ed[s][:, :], SH[:, s, 0, :], w2l, start=False, stop=False)
                nc.tensor.matmul(ed[s][:, :], SH[:, s, 0, :], w2h, start=False, stop=False)
                nc.tensor.matmul(ed[s][:, :], SL[0:64, s, 1, :], w2x[0:64, :], start=False, stop=False)
                nc.tensor.matmul(ed[s][:, :], SH[:, s, 1, :], w2x, start=False, stop=True).then_inc(s_D[s], 1)

            rows_t(0, 0)

            def body(e, q, first, n):
                pe.wait_ge(s_elo, e + 1)
                stand(pe)

                def pair(g, before):
                    rows_t(g, 1)
                    up(g, 0, q)
                    act_t(g - 1, 1)
                    down(g - 1, 0, before)
                    rows_t(g + 1, 0)
                    up(g, 1, q)
                    act_t(g, 0)
                    down(g - 1, 1, before)

                pair(first, (q - 1) % WSETS)
                with pe.Fori(1, n) as i:
                    pair(first + i, q)

            total = each_expert(pe, body)
            last = (EXPERTS - 1) % WSETS
            act_t(total - 1, 1)
            down(total - 1, 0, last)
            down(total - 1, 1, last)

        def moe_act(act):
            for s in range(2):
                for x in (s_exh, s_sg):
                    act.sem_inc(x[s], 1)
                act.sem_inc(s_y[s], 2)
                act.sem_inc(s_hh[s], 2 - s)

            def weights_high(e, q, piece):
                if piece == 0:
                    act.wait_ge(s_ewr, 64 * e + 64)
                at, n = PIECES[piece]
                to = q * WSET + (at if at < W13 else W2H if at == W13 else W2X)
                nc.scalar.activation(WB[:, to:to + n], RAW[:, at:at + n], ACT.Copy).then_inc(s_ehi, 1)

            def rows_high(g, s):
                act.wait_ge(s_T[s], g + 2)
                act.wait_ge(s_U[s], g + 1)
                nc.scalar.activation(XH[:, s, :, :].rearrange("p k n -> p (k n)"), et[s][:, :], ACT.Copy).then_inc(s_exh[s], 1)

            def silu(g, s):
                act.wait_ge(s_U[s], g + 2)
                act.wait_ge(s_h[s], g + 1)
                nc.scalar.activation(sg[:, s, :], eu[s][:, 0:FFN], ACT.Silu).then_inc(s_sg[s], 1)

            def act_high(g, s):
                act.wait_ge(s_H[s], g + 3)
                act.wait_ge(s_D[s], g + 2)
                nc.scalar.activation(SH[:, s, 0:2, :].rearrange("p k n -> p (k n)"), eh[s][:, 0:2 * P], ACT.Copy).then_inc(s_hh[s], 1)

            def weigh(g, s, e):
                act.wait_ge(s_D[s], g + 3)
                act.wait_ge(s_add[s], 16 * (g + 4))
                act.wait_ge(s_exl[s], g + 2)
                w = wring[:, s, bass.ds(slot_of(g), 1), bass.ds(e, 1)].rearrange("p a n -> p (a n)")
                nc.scalar.activation(yb[:, s, :], ed[s][:, :], ACT.Copy, scale=w).then_inc(s_y[s], 1)

            nc.scalar.activation(fnm[:, 0, 0:1], mhalf[:, :], ACT.Silu)
            act.wait_ge(s_q, 4 * TILES)
            for piece in range(len(PIECES)):
                weights_high(0, 0, piece)
            act.wait_ge(s_pad, 1)
            rows_high(0, 0)

            def body(e, q, first, n):
                more = not (isinstance(e, int) and e + 1 == EXPERTS)

                def pair(g, eb, split):
                    steps = (lambda: rows_high(g, 1), lambda: silu(g, 0), lambda: act_high(g - 1, 1),
                             lambda: weigh(g - 1, 0, eb), lambda: rows_high(g + 1, 0), lambda: silu(g, 1),
                             lambda: act_high(g, 0), lambda: weigh(g - 1, 1, eb))
                    for k, step in enumerate(steps):
                        step()
                        if split and k < len(PIECES):
                            weights_high(e + 1, (q + 1) % WSETS, k)

                pair(first, act.snap((e + EXPERTS - 1) & (EXPERTS - 1)) if not isinstance(e, int) else e - 1, more)
                with act.Fori(1, n) as i:
                    pair(first + i, e, False)

            total = each_expert(act, body)
            act_high(total - 1, 1)
            weigh(total - 1, 0, EXPERTS - 1)
            weigh(total - 1, 1, EXPERTS - 1)

            for p in range(FSTEPS // FRING):
                for r in range(FRING):
                    act.wait_ge(s_fnm, FRING * p + r + 1)
                    if r >= FOUT:
                        act.wait_ge(s_fst[r % FOUT], 16 * (2 * p + r // FOUT))
                    elif p:
                        act.wait_ge(s_fst[r % FOUT], 16 * (2 * p))
                    for j in range(2):
                        last = nc.scalar.activation(fn[:, r % FOUT, j, :], fa[:, r, j, :], ACT.Identity, bias=fnm[:, r, j:j + 1],
                                                    scale=frs[:, r, j:j + 1])
                    last.then_inc(s_fn, 1)

        def moe_dve(dve):
            dve.wait_ge(s_rk, 2 * TILES)
            dve.wait_ge(s_posf, TILES)
            nc.vector.tensor_copy(cnt_f, carry[0:1, :]).then_inc(s_tab, 1)
            dve.wait_ge(s_tab, 1)
            nc.vector.tensor_scalar(cnt_i, cnt_f, float(PAIR - 1), None, ALU.add).then_inc(s_tab, 1)
            dve.wait_ge(s_tab, 2)
            nc.vector.tensor_scalar(pr_i, cnt_i, PAIR.bit_length() - 1, None, ALU.arith_shift_right).then_inc(s_tab, 1)
            dve.wait_ge(s_tab, 3)
            nc.vector.tensor_scalar(pr_f, pr_i, 2.0, None, ALU.max).then_inc(s_tab, 1)
            nc.vector.memset(cnt_f, 0.0).then_inc(s_tab, 1)
            dve.wait_ge(s_tab, 5)
            nc.vector.tensor_copy(table[:, 0, :], pr_f)
            nc.vector.tensor_tensor_scan(inc_f, pr_f, cnt_f, 0.0, ALU.add, ALU.add).then_inc(s_tab, 1)
            dve.wait_ge(s_tab, 6)
            nc.vector.tensor_tensor(table[:, 1, :], inc_f, pr_f, ALU.subtract).then_inc(s_tabd, 1)
            dve.wait_ge(s_o, 4 * TILES)
            nc.vector.memset(SH[:, 0, 0:2, :].bitcast(f32), 0.0)
            nc.vector.memset(SL[:, 0, 0:2, :].bitcast(f32), 0.0)
            nc.vector.memset(WB[:, (WSETS - 1) * WSET + W2H:WSETS * WSET].bitcast(f32), 0.0)
            nc.vector.memset(hx[:, 1, :], 0.0).then_inc(s_tab, 1)
            dve.wait_ge(s_tab, 7)
            for s in range(2):
                for x in (s_exl, s_h, s_wr):
                    dve.sem_inc(x[s], 1)
                dve.sem_inc(s_hl[s], 2 - s)

            def weights_low(e, q, piece):
                dve.wait_ge(s_ehi, len(PIECES) * e + piece + 1)
                w = WB[:, q * WSET:(q + 1) * WSET]
                at, n = PIECES[piece]
                if at < W13:
                    low, high, rows = w[:, W13 + at:W13 + at + n], w[:, at:at + n], slice(0, P)
                elif at == W13:
                    low, high, rows = w[:, W2L:W2L + n], w[:, W2H:W2H + n], slice(0, P)
                else:
                    low, high, rows = w[64:P, W2X:W2X + n], w[64:P, W2X:W2X + n], slice(64, P)
                done = nc.vector.tensor_tensor(low, RAW[rows, at:at + n], high.bitcast(f32), ALU.subtract)
                if piece + 1 == len(PIECES):
                    done.then_inc(s_elo, 1)

            def rows_low(g, s):
                dve.wait_ge(s_ld[s], 16 * g + 16)
                nc.vector.tensor_copy(wring[:, s, bass.ds(slot_of(g), 1), :].rearrange("p a n -> p (a n)"),
                                      xr[:, s, W_COL:ROW]).then_inc(s_wr[s], 1)
                dve.wait_ge(s_exh[s], g + 2)
                hi = XH[:, s, :, :].rearrange("p k n -> p (k n)")
                nc.vector.tensor_tensor(XL[:, s, :, :].rearrange("p k n -> p (k n)"), et[s][:, :], hi.bitcast(f32),
                                        ALU.subtract).then_inc(s_exl[s], 1)

            def gate(g, s):
                dve.wait_ge(s_sg[s], g + 2)
                dve.wait_ge(s_H[s], g + 2)
                nc.vector.tensor_tensor(hx[:, s, 0:P], sg[:, s, 0:P], eu[s][:, FFN:FFN + P], ALU.mult)
                shape, twice = (P, 2, FFN - P), "p (a n) -> p a n"
                nc.vector.tensor_tensor(hx[:, s, P:2 * P].rearrange(twice, a=2),
                                        sg[:, s, P:FFN].rearrange(twice, a=1).to_broadcast(shape),
                                        eu[s][:, FFN + P:UP].rearrange(twice, a=1).to_broadcast(shape), ALU.mult).then_inc(s_h[s], 1)

            def act_low(g, s):
                dve.wait_ge(s_hh[s], g + 3)
                hi = SH[:, s, 0:2, :].rearrange("p k n -> p (k n)")
                nc.vector.tensor_tensor(SL[:, s, 0:2, :].rearrange("p k n -> p (k n)"), eh[s][:, 0:2 * P], hi.bitcast(f32),
                                        ALU.subtract).then_inc(s_hl[s], 1)

            for piece in range(len(PIECES)):
                weights_low(0, 0, piece)

            def body(e, q, first, n):
                more = not (isinstance(e, int) and e + 1 == EXPERTS)

                def pair(g, split):
                    steps = (lambda: rows_low(g, 1), lambda: gate(g, 0), lambda: act_low(g - 1, 1),
                             lambda: rows_low(g + 1, 0), lambda: gate(g, 1), lambda: act_low(g, 0))
                    for k, step in enumerate(steps):
                        step()
                        if split:
                            weights_low(e + 1, (q + 1) % WSETS, k)

                pair(first, more)
                with dve.Fori(1, n) as i:
                    pair(first + i, False)

            rows_low(0, 0)
            total = each_expert(dve, body)
            act_low(total - 1, 1)

            def stats(f, r):
                dve.wait_ge(s_fl[r], (f - r) * (16 // FRING) + 16)
                for j in range(2):
                    nc.vector.bn_stats(fbs[:, r, j, :], fa[:, r, j, :]).then_inc(s_fbs, 1)

            def aggregate(f, r):
                dve.wait_ge(s_fbs, 2 * f + 2)
                stand(dve)
                for j in range(2):
                    nc.vector.bn_aggr(fmv[:, r, j, :], fbs[:, r, j, :]).then_inc(s_fmv, 1)

            def shift(f, r):
                dve.wait_ge(s_frs, f + 1)
                nc.vector.scalar_tensor_tensor(fnm[:, r, :], fmv[:, r, :, 0], -1.0, frs[:, r, :], ALU.mult, ALU.mult).then_inc(s_fnm, 1)

            def add(f):
                dve.wait_ge(s_fn, f + 1)
                if f % XRING == 0:
                    dve.wait_ge(s_fx, 16 * min(f + XRING, FSTEPS))
                nc.vector.tensor_tensor(fn[:, f % FOUT, :, :], fx[:, f % XRING, :, :], fn[:, f % FOUT, :, :], ALU.add).then_inc(s_fo, 1)

            for f in range(FSTEPS):
                stats(f, f % FRING)
                if f >= 2:
                    add(f - 2)
                aggregate(f, f % FRING)
                if f >= 1:
                    shift(f - 1, (f - 1) % FRING)
            shift(FSTEPS - 1, (FSTEPS - 1) % FRING)
            add(FSTEPS - 2)
            add(FSTEPS - 1)

        def moe_pool(pool):
            pool.wait_ge(s_xn, 2 * TILES)
            nc.gpsimd.memset(wring, 0.0).then_inc(s_pad, 1)
            for s in range(2):
                nc.gpsimd.memset(yb[:, s, :], 0.0).then_inc(s_pad0, 1)
                nc.gpsimd.iota(idring[:, s, :], [[0, RING]], base=TRASH + s * P, channel_multiplier=1).then_inc(s_pad0, 1)
                nc.gpsimd.iota(aidx[:, s:s + 1], [[0, 1]], base=TRASH + s * P, channel_multiplier=1).then_inc(s_pad0, 1)
            pool.wait_ge(s_pad0, 6)

            def add_rows(s):
                nc.gpsimd.indirect_dma_start(acc_dram[:, :], bass.IndirectOffsetOnAxis(aidx[:, s:s + 1], 0), yb[:, s, :], None,
                                             compute_op=ALU.add).then_inc(s_add[s], 16)

            for s in range(2):
                add_rows(s)
            for i in range(2):
                pool.wait_ge(s_rst[i], TILES // 2 * 16)

            def add(g, s):
                pool.wait_ge(s_y[s], g + 4)
                if s == 0:
                    for i in range(2):
                        pool.wait_ge(s_add[i], 16 * (g + 4))
                nc.gpsimd.tensor_copy(aidx[:, s:s + 1], idring[:, s, bass.ds(slot_of(g), 1)]).then_inc(s_ai[s], 1)
                pool.wait_ge(s_ai[s], g + 4)
                stand(pool)
                add_rows(s)

            def gather(g, s, q, col):
                pool.wait_ge(s_T[s], g + 1)
                pool.wait_ge(s_wr[s], g + 1)
                src = lst[:, q, bass.ds(col, 1)]
                nc.gpsimd.tensor_copy(idring[:, s, bass.ds(slot_of(g), 1)], src)
                nc.gpsimd.tensor_copy(gidx[:, s:s + 1], src).then_inc(s_gi[s], 1)
                pool.wait_ge(s_gi[s], g + 1)
                stand(pool)
                nc.gpsimd.indirect_dma_start(xr[:, s, :], None, rows_dram[:, :], bass.IndirectOffsetOnAxis(gidx[:, s:s + 1], 0)
                                             ).then_inc(s_ld[s], 16)

            def body(e, q, first, n):
                pool.wait_ge(s_lst[q % 2], (e - q % 2) * 8 + 16)
                stand(pool)
                with pool.Fori(0, n) as i:
                    g = first + i
                    gather(g, 0, q % 2, 2 * i)
                    add(g - 3, 0)
                    gather(g, 1, q % 2, 2 * i + 1)
                    add(g - 3, 1)
                pool.sem_inc(s_lused, 1)

            total = each_expert(pool, body)
            gather(total, 0, 1, COLS - 1)
            for g in (total - 3, total - 2, total - 1):
                add(g, 0)
                add(g, 1)

            with pool.Fori(0, FSTEPS // FRING) as p:
                for r in range(FRING):
                    f = FRING * p + r
                    pool.wait_ge(s_fmv, 2 * f + 2)
                    stand(pool)
                    nc.gpsimd.tensor_scalar(fve[:, r, :], fmv[:, r, :, 1], NORM_EPS, None, ALU.add).then_inc(s_fve, 1)
                    pool.wait_ge(s_fve, f + 1)
                    nc.gpsimd.tensor_tensor(frs[:, r, :], fve[:, r, :], mhalf2[:, :], ALU.pow).then_inc(s_frs, 1)

        @block.sync
        def _(sp):
            def load_x(u, s, t):
                wait(sp, s_xn, u - 1)
                sp.dma_start(X[:, s, :], x_in[bass.ds(t * P, P), :]).then_inc(s_x[s], 16)

            load_x(0, 0, 0)
            sp.dma_start(raw2[0], wkv_in[0]).then_inc(s_raw[0], 16)
            sp.dma_start(raw2[1], wkv_in[1]).then_inc(s_raw[1], 16)
            load_x(1, 1, 1)
            sp.dma_start(bkv, bkv_in.to_broadcast((P, 2 * HID))).then_inc(s_bias, 16)
            for k in (2, 3):
                sp.wait_ge(s_wlo, k - 1)
                sp.dma_start(raw2[k % 2], wkv_in[k]).then_inc(s_raw[k % 2], 16)
            sp.dma_start(wg[:, :, :], wg_in.rearrange("(k p) n -> p k n", p=P)).then_inc(s_wg, 16)
            def a_body(u, s):
                if not (isinstance(u, int) and u + 2 > 31):
                    load_x(u + 2, s, u + 2)
                if isinstance(u, int) and u == 0:
                    sp.wait_ge(s_zero, 1)
                sp.dma_start(acc_dram[bass.ds(u * P, P), :], zero).then_inc(s_zeroed, 16)
                if isinstance(u, int) and u < 16:
                    return
                if s_wq_on[0]:
                    wait(sp, s_wlo, KC + u - 17)
                    sp.dma_start(raw2[s][:, 0:HID], wq_in[bass.ds(u - 16, 1), :, :].rearrange("a p n -> p (a n)")
                                 ).then_inc(s_raw[s], 16)

            s_wq_on = [False]
            a_body(0, 0)
            a_body(1, 1)
            a_body(2, 0)
            a_body(3, 1)
            sp.wait_ge(s_trash, 1)
            sp.dma_start(lists.rearrange("(e p q) a -> p e (q a)", e=EXPERTS, p=P),
                         trash.rearrange("p (e q) -> p e q", e=EXPERTS)).then_inc(s_lists, 16)
            for b in range(TOKENS // P, (TOKENS + PAIR) // P):
                sp.dma_start(acc_dram[b * P:(b + 1) * P, :], zero).then_inc(s_zeroed, 16)
                sp.dma_start(rows_dram[b * P:(b + 1) * P, 0:HID], zero).then_inc(s_zeroed, 16)
                sp.dma_start(rows_dram[b * P:(b + 1) * P, HID:ROW], zero[:, 0:EXPERTS]).then_inc(s_zeroed, 16)
            pairs_of(4, 16, sp, a_body)
            sp.wait_ge(s_lists, 16)
            sp.dma_start(bq[:, :], bq_in.to_broadcast((P, HEADS * HEAD_DIM))).then_inc(s_wg, 16)
            s_wq_on[0] = True
            a_body(16, 0)
            a_body(17, 1)
            pairs_of(18, 30, sp, a_body)
            a_body(30, 0)
            a_body(31, 1)
            load_x(TILES, 0, 0)
            load_x(TILES + 1, 1, 1)

            def load_wo(b):
                for c in range(HEADS // 2):
                    if b == 0 and c < 2:
                        sp.wait_ge(s_wlo, KC + 15 + c)
                    else:
                        sp.wait_ge(s_m, HEADS * b + 2 * c - 2)
                    sp.dma_start(raw2[c % 2].rearrange("p (a n) -> p a n", a=2),
                                 wo_in[2 * c:2 * c + 2, :, :].rearrange("a p n -> p a n")).then_inc(s_raw[c % 2], 16)

            def b_body(t, s, b):
                if live(t, 2):
                    sp.wait_ge(s_x2, t - 1)
                    sp.dma_start(x2_dram[bass.ds((t - 2) * P, P), :], XRES[:, s, :]).then_inc(s_x2st[s], 16)
                if live(t, 3):
                    sp.wait_ge(s_wd, t - 2)
                    sp.dma_start(rows_dram[bass.ds((t - 3) * P, P), :], row[:, 1 - s, :]).then_inc(s_rst[1 - s], 16)
                if isinstance(t, int) and t + 2 < TILES or not isinstance(t, int):
                    load_x(t + TILES + 2, s, t + 2)
                if live(t):
                    if not (isinstance(t, int) and t < 2):
                        sp.wait_ge(s_x2st[s], (t - s) * 8)
                        sp.wait_ge(s_row, t - 1)
                    sp.dma_start(XRES[:, s, :], x_in[bass.ds(t * P, P), :]).then_inc(s_xres[s], 16)

            b_body(0, 0, 0)
            load_wo(0)
            for t in (1, 2, 3):
                b_body(t, t % 2, 0)
            pairs_of(4, 16, sp, lambda t, s: b_body(t, s, 0))
            load_wo(1)
            b_body(16, 0, 1)
            b_body(17, 1, 1)
            pairs_of(18, 30, sp, lambda t, s: b_body(t, s, 1))
            for t in range(30, 35):
                b_body(t, t % 2, 1)
            moe_sp(sp)

        @block.tensor
        def _(pe):
            def split_matmuls(ps, terms, start=True, stop=True):
                for i, (w, m) in enumerate(terms):
                    last = nc.tensor.matmul(ps, w, m, start=start and i == 0, stop=stop and i == len(terms) - 1)
                return last

            def three(wh, wl, mh, ml):
                return [(wl, mh), (wh, ml), (wh, mh)]

            def t_x(u, s):
                pe.wait_ge(s_xn, u + 1)
                wait(pe, s_xl, u)
                if isinstance(u, int) and u in (TILES + 2, TILES + BATCH_TILES + 2):
                    pe.wait_ge(s_ktc, 1 + (u - TILES) // BATCH_TILES)
                for k in range(KC):
                    last = nc.tensor.transpose(pt[:, k * P:(k + 1) * P], XN[:, k * P:(k + 1) * P], ident[:, :])
                last.then_inc(s_xt, 1)

            def kv_tile(u, s):
                wait(pe, s_z, u - 1)
                pe.wait_ge(s_xl, u + 1)
                for c, (ps, done) in enumerate(((pk[s], s_k), (pv[s], s_v))):
                    if c:
                        t_x(u + 1, 1 - s)
                    terms = []
                    for k in range(KC):
                        cols = slice(k * 2 * HID + c * HID, k * 2 * HID + (c + 1) * HID)
                        terms += three(XH[:, s, k, :], XL[:, s, k, :], wkv_hi[:, cols], wkv_lo[:, cols])
                    if c:
                        wait(pe, s_vx, u - 1)
                    split_matmuls(ps[:, :], terms).then_inc(done, 1)

            def kv_clear(b):
                wait(pe, s_kvev, b)
                for i in range(2):
                    nc.tensor.matmul(pkv[i][:, :], zero[:, 0:P], zero, start=True, stop=False, skip_group_check=True)

            def kv_add(u, s, stop=False):
                pe.wait_ge(s_sk, u + 1)
                pe.wait_ge(s_vx, u + 1)
                n = HEAD_DIM + 1
                for h in range(KV_HEADS):
                    last = nc.tensor.matmul(pkv[h // 2][:, (h % 2) * 256:(h % 2) * 256 + n], sk[:, s, h * P:(h + 1) * P],
                                            vx[:, s, h, 0:n], start=False, stop=stop, skip_group_check=True)
                last.then_inc(s_acc, 1)

            def a_body(u, s):
                kv_tile(u, s)
                if isinstance(u, int) and u == 0:
                    return
                if isinstance(u, int) and u in (1, 17):
                    kv_clear(u // 16)
                kv_add(u - 1, 1 - s, stop=isinstance(u, int) and u == 16)

            pe.wait_ge(s_const, 1)
            pe.wait_ge(s_consts2, 4)
            pe.wait_ge(s_zero, 1)
            t_x(0, 0)
            pe.wait_ge(s_wlo, KC)
            run_a(pe, a_body)
            kv_add(TILES - 1, 1, stop=True)

            for b in range(BATCH):
                pe.wait_ge(s_diag, KV_HEADS * (b + 1))
                wait(pe, s_ksum, b)
                nc.tensor.matmul(pr[:, :], ones[:, :], prod, start=True, stop=True).then_inc(s_ksb, 1)

            pe.wait_ge(s_wlo, KC + 16)
            pe.wait_ge(s_wg, 32)

            def fold(b):
                pe.wait_ge(s_xl, TILES + BATCH_TILES * b + 2)
                for h in range(KV_HEADS):
                    last = nc.tensor.transpose(pt[:, h * P:(h + 1) * P], kvs[b][:, h, 0:HEAD_DIM], ident[:, :])
                last.then_inc(s_kt, 1)
                pe.wait_ge(s_ktc, b + 1)
                pe.wait_ge(s_zq, 64 * b + 4)
                for h in range(HEADS):
                    if h >= 2:
                        pe.wait_ge(s_mlo, HEADS * b + h - 1)
                    if h % 2 == 0:
                        base = (KC // 2 + 8 + 4 * b) * 16
                        pe.wait_ge(s_raw[h // 2 % 2], base + 16 * (h // 4 + 1))
                    nc.tensor.matmul(pq[h % 2][:, :], kvt[:, h // GROUP, :], raw2[h // 2 % 2][:, (h % 2) * HID:(h % 2 + 1) * HID],
                                     start=True, stop=True).then_inc(s_m, 1)
                pe.wait_ge(s_mlo, HEADS * (b + 1))

            def b_body(t, s, b):
                fixed = isinstance(t, int)
                for c in range(CHUNKS):
                    j = 4 * t + c
                    if live(t):
                        if c == 0:
                            pe.wait_ge(s_xl, t + TILES + 1)
                        wait(pe, s_zq, j - 1)
                        terms = []
                        for k in range(KC):
                            cols = slice(k * HEADS * P + c * HID, k * HEADS * P + (c + 1) * HID)
                            terms += three(XH[:, s, k, :], XL[:, s, k, :], wq_hi[:, cols], wq_lo[:, cols])
                        split_matmuls(pq[c % 2][:, :], terms).then_inc(s_q, 1)
                    if not fixed or 0 <= j - 2 < 4 * TILES:
                        i = (c - 2) % 2
                        pe.wait_ge(s_scale, j - 1)
                        wait(pe, s_slo, j - 3)
                        for h in range(GROUP):
                            last = nc.tensor.transpose(pst[i][:, h * P:(h + 1) * P], sqn[:, i, h * P:(h + 1) * P], ident[:, :])
                        last.then_inc(s_st, 1)
                    if c == 2 and (not fixed or t + 1 < TILES):
                        t_x(t + TILES + 1, 1 - s)
                    if fixed and c == 3 and t in (0, BATCH_TILES):
                        fold(b)
                    if not fixed or 0 <= j - 3 < 4 * TILES:
                        i, cc = (c - 3) % 2, (c - 3) % 4
                        tile_parity = s if c == 3 else 1 - s
                        ot = t if c == 3 else t - 1
                        pe.wait_ge(s_slo, j - 2)
                        if cc == 0:
                            wait(pe, s_on, ot - 1)
                        terms = []
                        for h in range(GROUP):
                            cols = slice((cc * GROUP + h) * HID, (cc * GROUP + h + 1) * HID)
                            terms += three(SH[:, i, h, :], SL[:, i, h, :], m_hi[:, cols], m_lo[:, cols])
                        split_matmuls(po[tile_parity][:, :], terms, start=cc == 0, stop=cc == 3).then_inc(s_o, 1)
                    if c == 3 and live(t, 2):
                        pe.wait_ge(s_row, t - 1)
                        wait(pe, s_rk, 2 * t - 4)
                        for k in range(KC):
                            last = nc.tensor.transpose(pr[:, k * P:(k + 1) * P], row[:, s, k * P:(k + 1) * P], ident[:, :])
                        last.then_inc(s_rt, 1)
                    if c == 0 and live(t, 3):
                        pe.wait_ge(s_x2t, t - 2)
                        for k in range(KC):
                            last = nc.tensor.matmul(pr[:, 0:EXPERTS], x2t[:, k, :], wg[:, k, :], start=k == 0, stop=k == KC - 1)
                        last.then_inc(s_lgt, 1)
                    if c == 2 and live(t, 3):
                        pe.wait_ge(s_msk, t - 2)
                        pe.wait_ge(s_lg, t - 2)
                        nc.tensor.matmul(pr[:, 64:64 + EXPERTS], upper[:, :], msk[:, :], start=True, stop=True)
                        nc.tensor.matmul(pr[:, 128:128 + EXPERTS], ones[:, :], msk[:, :], start=True,
                                         stop=True).then_inc(s_rank, 1)

            run_b(pe, b_body)
            moe_pe(pe)

        @block.scalar
        def _(act):
            def x_high(u, s, free, at_least):
                act.wait_ge(s_xt, u + 1)
                wait(act, free, at_least)
                nc.scalar.activation(XH[:, s, :, :].rearrange("p k n -> p (k n)"), pt[:, :], ACT.Copy).then_inc(s_xh, 1)

            def x_norm(u, s):
                act.wait_ge(s_rs, u + 1)
                wait(act, s_xt, u)
                nc.scalar.activation(XN[:, :], X[:, s, :], ACT.Identity, bias=nmr[:, 0:1], scale=rs[:, 0:1]).then_inc(s_xn, 1)

            def w_high(dst, src, sem_loaded, value):
                act.wait_ge(sem_loaded, value)
                nc.scalar.activation(dst, src, ACT.Copy).then_inc(s_whi, 1)

            x_norm(0, 0)
            for k in range(KC):
                w_high(wkv_hi[:, k * 1024:(k + 1) * 1024], raw2[k % 2], s_raw[k % 2], 16 * (k // 2 + 1))
            x_high(0, 0, s_v, 0)
            x_norm(1, 1)

            def a_body(u, s):
                x_high(u + 1, 1 - s, s_v, u)
                act.wait_ge(s_z, u + 1)
                wait(act, s_sk, u)
                nc.scalar.activation(ek, zk, ACT.Relu, scale=-1.0).then_inc(s_nr, 1)
                act.wait_ge(s_nr, u + 1)
                nc.scalar.activation(ek, ek, ACT.Exp, scale=-1.0).then_inc(s_e, 1)
                if not (isinstance(u, int) and u == TILES - 1):
                    x_norm(u + 2, s)
                if isinstance(u, int) and u == 16:
                    kv_out(0)
                if not isinstance(u, int) and not second[0]:
                    return
                if isinstance(u, int) and u < 16:
                    return
                w_high(wq_hi[:, bass.ds((u - 16) * HID, HID)], raw2[s][:, 0:HID], s_raw[s], 16 * (KC // 2) + (u - 16 - s) * 8 + 16)

            def kv_out(b):
                act.wait_ge(s_acc, BATCH_TILES * (b + 1))
                for i in range(2):
                    last = nc.scalar.activation(kvs[b][:, 2 * i:2 * i + 2, :],
                                                pkv[i][:, :].rearrange("p (h n) -> p h n", h=2)[:, :, 0:HEAD_DIM + 1], ACT.Copy)
                last.then_inc(s_kvev, 1)

            second = [False]
            a_body(0, 0)
            a_body(1, 1)
            pairs_of(2, 16, act, a_body)
            second[0] = True
            a_body(16, 0)
            a_body(17, 1)
            pairs_of(18, 30, act, a_body)
            a_body(30, 0)
            a_body(31, 1)
            kv_out(1)

            def fold(b):
                act.wait_ge(s_kt, b + 1)
                nc.scalar.activation(kvt[:, :, :].rearrange("p h n -> p (h n)"), pt[:, :], ACT.Copy).then_inc(s_ktc, 1)
                for h in range(HEADS):
                    act.wait_ge(s_m, HEADS * b + h + 1)
                    nc.scalar.activation(m_hi[:, h * HID:(h + 1) * HID], pq[h % 2][:, :], ACT.Copy).then_inc(s_mhi, 1)

            def b_body(t, s, b):
                fixed = isinstance(t, int)
                for c in range(CHUNKS):
                    j = 4 * t + c
                    if c == 0 and live(t, 3):
                        act.wait_ge(s_rt, t - 2)
                        wait(act, s_lgt, t - 3)
                        nc.scalar.activation(x2t[:, :, :].rearrange("p k n -> p (k n)"), pr[:, :], ACT.Copy).then_inc(s_x2t, 1)
                    if not fixed or 0 <= j - 2 < 4 * TILES:
                        i = (c - 2) % 2
                        act.wait_ge(s_st, j - 1)
                        wait(act, s_o, j - 3)
                        nc.scalar.activation(SH[:, i, :, :].rearrange("p h n -> p (h n)"), pst[i][:, :],
                                             ACT.Copy).then_inc(s_shi, 1)
                    if c == 1 and (not fixed or t + 1 < TILES):
                        x_norm(t + TILES + 1, 1 - s)
                    if fixed and c == 3 and t in (0, BATCH_TILES):
                        fold(b)
                    if live(t):
                        act.wait_ge(s_zq, j + 1)
                        wait(act, s_sq, j - 1)
                        nc.scalar.activation(e[:, c % 2, :], z[:, c % 2, :], ACT.Relu, scale=-1.0).then_inc(s_nq, 1)
                        act.wait_ge(s_nq, j + 1)
                        nc.scalar.activation(e[:, c % 2, :], e[:, c % 2, :], ACT.Exp, scale=-1.0).then_inc(s_eq, 1)
                    if c == 2 and (not fixed or t + 1 < TILES):
                        if fixed and t == 0:
                            x_high(TILES + 1, 1, s_v, TILES)
                        else:
                            x_high(t + TILES + 1, 1 - s, s_q, 4 * t)
                    if c == 1 and live(t, 2):
                        act.wait_ge(s_2rs, t - 1)
                        wait(act, s_rst[s], (t - 2 - s) * 8)
                        nc.scalar.activation(row[:, s, 0:HID], XRES[:, s, :], ACT.Identity, bias=nmr[:, 2:3],
                                             scale=rs[:, 2:3]).then_inc(s_row, 1)
                    if c == 2 and live(t, 3):
                        act.wait_ge(s_nmx, t - 2)
                        wait(act, s_wun, t - 3)
                        nc.scalar.activation(ex[:, :], lg[:, :], ACT.Exp, bias=negmax[:, 0:1]).then_inc(s_ex, 1)
                    if c == 3 and live(t, 1):
                        act.wait_ge(s_ors, t)
                        wait(act, s_x2, t - 1)
                        nc.scalar.activation(on, po[1 - s][:, :], ACT.Identity, bias=nmr[:, 1:2], scale=rs[:, 1:2]).then_inc(s_on, 1)
                    if live(t):
                        act.wait_ge(s_rec, j + 1)
                        wait(act, s_st, j - 1)
                        for h in range(GROUP):
                            last = nc.scalar.activation(sqn[:, c % 2, h * P:(h + 1) * P], sq[:, c % 2, h * P:(h + 1) * P],
                                                        ACT.Copy, scale=rec[:, c % 2, h:h + 1])
                        last.then_inc(s_scale, 1)

            act.wait_ge(s_zeroed, 16 * (TOKENS // P + 3 * PAIR // P))
            run_b(act, b_body)
            moe_act(act)

        @block.vector
        def _(dve):
            nc.vector.memset(ones[:, :], 1.0)
            nc.vector.memset(zero, 0.0).then_inc(s_zero, 1)
            nc.vector.memset(vx[:, :, :, HEAD_DIM:HEAD_DIM + 2], 1.0)
            nc.vector.memset(mhalf2[:, :], -0.5)
            nc.vector.memset(mhalf[:, :], -0.5).then_inc(s_const, 1)

            def mean_var(src, slot, s_stats, s_out, n, s_used):
                wait(dve, s_used, n - 1)
                nc.vector.bn_stats(bst[:, slot, :], src).then_inc(s_stats, 1)
                dve.wait_ge(s_stats, n)
                stand(dve)
                nc.vector.bn_aggr(mv[:, slot, :], bst[:, slot, :]).then_inc(s_out, 1)

            def x_stats(u, s, loads):
                dve.wait_ge(s_x[s], 16 * loads)
                mean_var(X[:, s, :], 0, s_bs, s_mv, u + 1, s_rs)

            def x_low(u, s):
                dve.wait_ge(s_xh, u + 1)
                hi = XH[:, s, :, :].rearrange("p k n -> p (k n)")
                nc.vector.tensor_tensor(XL[:, s, :, :].rearrange("p k n -> p (k n)"), pt[:, :], hi.bitcast(f32),
                                        ALU.subtract).then_inc(s_xl, 1)

            def w_low(lo, hi, src, n):
                dve.wait_ge(s_whi, n)
                nc.vector.tensor_tensor(lo, src, hi.bitcast(f32), ALU.subtract).then_inc(s_wlo, 1)

            x_stats(0, 0, 1)
            for k in range(KC):
                w_low(wkv_lo[:, k * 1024:(k + 1) * 1024], wkv_hi[:, k * 1024:(k + 1) * 1024], raw2[k % 2], k + 1)
            x_low(0, 0)
            x_stats(1, 1, 1)
            dve.wait_ge(s_bias, 16)

            def a_body(u, s):
                dve.wait_ge(s_k, u + 1)
                wait(dve, s_sk, u)
                nc.vector.tensor_tensor(zk, pk[s][:, :], bkv[:, 0:HID], ALU.add).then_inc(s_z, 1)
                x_low(u + 1, 1 - s)
                if not (isinstance(u, int) and u == TILES - 1):
                    dve.wait_ge(s_x[s], (u - s) * 8 + 32)
                    mean_var(X[:, s, :], 0, s_bs, s_mv, u + 3, s_rs)
                wait(dve, s_acc, u - 1)
                dve.wait_ge(s_e, u + 1)
                nc.vector.scalar_tensor_tensor(sk[:, s, :], zk, 1.0, ek, ALU.add, ALU.max).then_inc(s_sk, 1)
                dve.wait_ge(s_v, u + 1)
                nc.vector.tensor_tensor(vx[:, s, :, 0:HEAD_DIM], pv[s][:, :].rearrange("p (h n) -> p h n", h=KV_HEADS),
                                        bkv[:, HID:2 * HID].rearrange("p (h n) -> p h n", h=KV_HEADS), ALU.add).then_inc(s_vx, 1)
                if (isinstance(u, int) and u < 16) or not second[0]:
                    return
                cols = bass.ds((u - 16) * HID, HID)
                w_low(wq_lo[:, cols], wq_hi[:, cols], raw2[s][:, 0:HID], KC + u - 15)

            second = [False]
            a_body(0, 0)
            a_body(1, 1)
            pairs_of(2, 16, dve, a_body)
            second[0] = True
            a_body(16, 0)
            a_body(17, 1)
            pairs_of(18, 30, dve, a_body)
            a_body(30, 0)
            a_body(31, 1)

            dve.wait_ge(s_consts2, 7)
            for b in range(BATCH):
                dve.wait_ge(s_kvev, BATCH)
                wait(dve, s_ksb, b)
                for h in range(KV_HEADS):
                    nc.vector.tensor_scalar(prod[:, h * P:(h + 1) * P], ident[:, :], kvs[b][:, h, HEAD_DIM:HEAD_DIM + 1], None,
                                            ALU.mult).then_inc(s_diag, 1)
                dve.wait_ge(s_ksb, b + 1)
                nc.vector.tensor_copy(ksumb[b][:, :], pr[:, :]).then_inc(s_ksum, 1)

            dve.wait_ge(s_wg, 32)

            def fold(b):
                for h in range(HEADS):
                    dve.wait_ge(s_mhi, HEADS * b + h + 1)
                    cols = slice(h * HID, (h + 1) * HID)
                    nc.vector.tensor_tensor(m_lo[:, cols], pq[h % 2][:, :], m_hi[:, cols].bitcast(f32), ALU.subtract).then_inc(s_mlo, 1)

            def norm_rec(j, i, b, c):
                dve.wait_ge(s_sq, j + 1)
                for h in range(GROUP):
                    cols = slice(h * P, (h + 1) * P)
                    nc.vector.tensor_tensor_reduce(prod[:, cols], sq[:, i, cols], ksumb[b][:, c * P:(c + 1) * P], 1.0, ATTN_EPS,
                                                   ALU.mult, ALU.add, nrm[:, h:h + 1]).then_inc(s_red, 1)
                dve.wait_ge(s_red, GROUP * j + GROUP)
                nc.vector.reciprocal(rec[:, i, :], nrm[:, :]).then_inc(s_rec, 1)

            def route(t, s):
                dve.wait_ge(s_lgt, t + 1)
                wait(dve, s_ex, t)
                nc.vector.tensor_copy(lg[:, :], pr[:, 0:EXPERTS]).then_inc(s_lg, 1)
                dve.wait_ge(s_lg, t + 1)
                stand(dve)
                nc.vector.max(mx8[:, :], lg[:, :]).then_inc(s_mx, 1)
                dve.wait_ge(s_mx, t + 1)
                nc.vector.tensor_scalar(negmax[:, :], mx8[:, 0:1], -1.0, None, ALU.mult).then_inc(s_nmx, 1)
                nc.vector.max_index(ix8[:, :], mx8[:, :], lg[:, :]).then_inc(s_ix, 1)
                dve.wait_ge(s_ix, t + 1)
                wait(dve, s_ri, 2 * t - 2)
                nc.vector.tensor_copy(ixf[:, s, :], ix8[:, :]).then_inc(s_ixf, 1)
                dve.wait_ge(s_ixf, t + 1)
                wait(dve, s_posf, t)
                nc.vector.tensor_tensor(oh[:, :, :], ixf[:, s, :].rearrange("p (k a) -> p k a", a=1).to_broadcast((P, TOP_K, EXPERTS)),
                                        iota_e[:, :].rearrange("p (a n) -> p a n", a=1).to_broadcast((P, TOP_K, EXPERTS)),
                                        ALU.is_equal).then_inc(s_oh, 1)
                dve.wait_ge(s_oh, t + 1)
                wait(dve, s_rank, t)
                wait(dve, s_wun, t)
                nc.vector.tensor_reduce(msk[:, :], oh[:, :, :].rearrange("p k n -> p n k"), AX.X, ALU.add).then_inc(s_msk, 1)

            def ranks(t):
                dve.wait_ge(s_rank, t + 1)
                wait(dve, s_rk, 2 * t)
                nc.vector.tensor_tensor(rank[:, :], pr[:, 64:64 + EXPERTS], carry[:, :], ALU.add).then_inc(s_rk, 1)
                dve.wait_ge(s_rk, 2 * t + 1)
                nc.vector.tensor_tensor(carry[:, :], pr[:, 128:128 + EXPERTS], carry[:, :], ALU.add).then_inc(s_rk, 1)

            def place(t, s):
                dve.wait_ge(s_ex, t + 1)
                dve.wait_ge(s_msk, t + 1)
                nc.vector.tensor_tensor(wun[:, :], ex[:, :], msk[:, :], ALU.mult).then_inc(s_wun, 1)
                dve.wait_ge(s_wun, t + 1)
                nc.vector.reduce_sum(wsum[:, :], wun[:, :], AX.X).then_inc(s_wsum, 1)
                dve.wait_ge(s_wsum, t + 1)
                nc.vector.reciprocal(wrec[:, :], wsum[:, :]).then_inc(s_wrec, 1)
                nc.vector.tensor_tensor(oh[:, :, :], oh[:, :, :],
                                        rank[:, :].rearrange("p (a n) -> p a n", a=1).to_broadcast((P, TOP_K, EXPERTS)),
                                        ALU.mult).then_inc(s_pf, 1)
                dve.wait_ge(s_wrec, t + 1)
                nc.vector.tensor_scalar(row[:, s, W_COL:W_COL + EXPERTS], wun[:, :], wrec[:, 0:1], None, ALU.mult).then_inc(s_wd, 1)
                dve.wait_ge(s_pf, t + 1)
                wait(dve, s_ci, 2 * t)
                nc.vector.reduce_sum(posf[:, :], oh[:, :, :], AX.X).then_inc(s_posf, 1)

            def list_places(t, s):
                wait(dve, s_id, 2 * t)
                wait(dve, s_sc[s], (t - s) * 64)
                nc.vector.tensor_copy(ids[:, s, :], idf[:, :]).then_inc(s_id, 1)
                dve.wait_ge(s_id, 2 * t + 1)
                nc.vector.tensor_scalar(idf[:, :], idf[:, :], float(P), None, ALU.add).then_inc(s_id, 1)
                dve.wait_ge(s_posf, t + 1)
                nc.vector.tensor_copy(rank_i[:, :], posf[:, :]).then_inc(s_ri, 1)
                nc.vector.tensor_scalar(at_f[:, :], ixf[:, s, :], float(CAP), None, ALU.mult).then_inc(s_ri, 1)
                dve.wait_ge(s_ri, 2 * t + 2)
                nc.vector.tensor_scalar(col_i[:, :], rank_i[:, :], P.bit_length() - 1, None, ALU.arith_shift_right).then_inc(s_ci, 1)
                nc.vector.scalar_tensor_tensor(at_f[:, :], posf[:, :], float(COLS), at_f[:, :], ALU.mult, ALU.add).then_inc(s_ci, 1)
                dve.wait_ge(s_ci, 2 * t + 2)
                nc.vector.tensor_copy(col_f[:, :], col_i[:, :]).then_inc(s_cf, 1)
                dve.wait_ge(s_cf, t + 1)
                nc.vector.scalar_tensor_tensor(pos[:, s, :], col_f[:, :], float(1 - P * COLS), at_f[:, :], ALU.mult, ALU.add).then_inc(s_pos, 1)

            def b_body(t, s, b):
                fixed = isinstance(t, int)
                for c in range(CHUNKS):
                    j = 4 * t + c
                    i = c % 2
                    if c == 3 and live(t, 3):
                        ranks(t - 3)
                    if live(t):
                        dve.wait_ge(s_q, j + 1)
                        nc.vector.tensor_tensor(z[:, i, :], pq[i][:, :], bq[:, c * HID:(c + 1) * HID], ALU.add).then_inc(s_zq, 1)
                    if not fixed or 0 <= j - 2 < 4 * TILES:
                        dve.wait_ge(s_shi, j - 1)
                        nc.vector.tensor_tensor(SL[:, i, :, :].rearrange("p h n -> p (h n)"), pst[i][:, :],
                                                SH[:, i, :, :].rearrange("p h n -> p (h n)").bitcast(f32), ALU.subtract).then_inc(s_slo, 1)
                    if fixed and c == 3 and t in (0, BATCH_TILES):
                        fold(b)
                    if c == 0 and (not fixed or t + 1 < TILES):
                        dve.wait_ge(s_x[1 - s], 16 * (TILES // 2) + (t + 1 - (1 - s)) * 8 + 16)
                        mean_var(X[:, 1 - s, :], 0, s_bs, s_mv, t + TILES + 2, s_rs)
                    if c == 0 and live(t, 2):
                        dve.wait_ge(s_x2, t - 1)
                        mean_var(XRES[:, s, :], 2, s_2bs, s_2mv, t - 1, s_2rs)
                    if c == 3 and live(t, 1):
                        dve.wait_ge(s_o, 4 * t)
                        mean_var(po[1 - s][:, :], 1, s_obs, s_omv, t, s_ors)
                    if live(t):
                        dve.wait_ge(s_eq, j + 1)
                        wait(dve, s_scale, j - 1)
                        nc.vector.scalar_tensor_tensor(sq[:, i, :], z[:, i, :], 1.0, e[:, i, :], ALU.add, ALU.max).then_inc(s_sq, 1)
                        norm_rec(j, i, b, c)
                    if c == 2 and (not fixed or t + 1 < TILES):
                        x_low(t + TILES + 1, 1 - s)
                    if c == 0 and live(t, 4):
                        list_places(t - 4, s)
                    if c == 1 and live(t, 3):
                        route(t - 3, 1 - s)
                    if c == 3 and live(t, 3):
                        place(t - 3, 1 - s)

            run_b(dve, b_body)
            moe_dve(dve)

        @block.gpsimd
        def _(pool):
            nc.gpsimd.memset(ident[:, :], 0.0).then_inc(s_consts2, 1)
            nc.gpsimd.memset(upper[:, :], 1.0).then_inc(s_consts2, 1)
            pool.wait_ge(s_consts2, 2)
            nc.gpsimd.affine_select(out=ident[:, :], in_=ident[:, :], compare_op=ALU.not_equal, fill=1.0, base=0,
                                    pattern=[[-1, P]], channel_multiplier=1).then_inc(s_consts2, 1)
            nc.gpsimd.affine_select(out=upper[:, :], in_=upper[:, :], compare_op=ALU.is_gt, fill=0.0, base=0,
                                    pattern=[[1, P]], channel_multiplier=-1).then_inc(s_consts2, 1)

            def rstd(slot, s_in, s_mid, s_out, n, s_used):
                wait(pool, s_used, n - 1)
                pool.wait_ge(s_in, n)
                stand(pool)
                nc.gpsimd.tensor_scalar(ve[:, slot:slot + 1], mv[:, slot, 1:2], NORM_EPS, None, ALU.add).then_inc(s_mid, 1)
                pool.wait_ge(s_mid, 2 * n - 1)
                nc.gpsimd.tensor_tensor(rs[:, slot:slot + 1], ve[:, slot:slot + 1], mhalf[:, :], ALU.pow).then_inc(s_mid, 1)
                pool.wait_ge(s_mid, 2 * n)
                stand(pool)
                nc.gpsimd.tensor_scalar(nmr[:, slot:slot + 1], mv[:, slot, 0:1], rs[:, slot:slot + 1], -1.0, ALU.mult,
                                        ALU.mult).then_inc(s_out, 1)

            nc.gpsimd.iota(trash, [[0, EXPERTS], [0, COLS // 2], [P, 2]], base=TRASH, channel_multiplier=1).then_inc(s_trash, 1)
            pool.wait_ge(s_const, 1)
            rstd(0, s_mv, s_ve, s_rs, 1, s_xn)
            nc.gpsimd.iota(iota_e[:, :], [[1, EXPERTS]], base=0, channel_multiplier=0, allow_small_or_imprecise_dtypes=True).then_inc(s_consts2, 1)
            nc.gpsimd.iota(carry[:, :], [[0, EXPERTS]], base=0, channel_multiplier=0, allow_small_or_imprecise_dtypes=True).then_inc(s_consts2, 1)
            nc.gpsimd.iota(idf[:, :], [[0, 1]], base=0, channel_multiplier=1, allow_small_or_imprecise_dtypes=True).then_inc(s_consts2, 1)
            rstd(0, s_mv, s_ve, s_rs, 2, s_xn)
            with pool.Fori(2, TILES + 1) as u:
                rstd(0, s_mv, s_ve, s_rs, u + 1, s_xn)

            pool.wait_ge(s_ksum, 2)
            pool.wait_ge(s_lists, 16)
            def send(t, s, k0, k1):
                if k0 == 0:
                    pool.wait_ge(s_pos, t + 1)
                    pool.wait_ge(s_id, 2 * t + 1)
                    stand(pool)
                for k in range(k0, k1):
                    nc.gpsimd.indirect_dma_start(lists[:, :], bass.IndirectOffsetOnAxis(pos[:, s, k:k + 1], 0), ids[:, s, :],
                                                 None).then_inc(s_sc[s], 16)

            def b_body(t, s, b):
                fixed = isinstance(t, int)
                for c in range(CHUNKS):
                    if c == 0 and live(t, 2):
                        pool.wait_ge(s_on, t - 1)
                        pool.wait_ge(s_xres[s], (t - 2 - s) * 8 + 16)
                        nc.gpsimd.tensor_tensor(XRES[:, s, :], XRES[:, s, :], on, ALU.add).then_inc(s_x2, 1)
                    if c == 0 and (not fixed or t + 1 < TILES):
                        rstd(0, s_mv, s_ve, s_rs, t + TILES + 2, s_xn)
                    if c == 0 and live(t, 2):
                        rstd(2, s_2mv, s_2ve, s_2rs, t - 1, s_row)
                    if c == 3 and live(t, 1):
                        rstd(1, s_omv, s_ove, s_ors, t, s_on)
                    if c > 0 and live(t, 4):
                        send(t - 4, s, 3 * c - 3, min(3 * c, TOP_K))

            run_b(pool, b_body)
            moe_pool(pool)


def kernel(**inputs):
    import numpy as np
    import concourse.bacc as bacc
    from concourse.bass_utils import run_bass_kernel_spmd

    a = {k: np.asarray(v) for k, v in inputs.items()}
    w_kv = np.concatenate([a["L0_attn_Wk"], a["L0_attn_Wv"]], 0).T
    w_13 = np.concatenate([a["L0_ffn_w1"], a["L0_ffn_v1"]], 2)
    arrays = {
        "x_in": a["L0_attn_hidden_states"].reshape(TOKENS, HID),
        "wkv_in": w_kv.reshape(KC, P, 2 * HID),
        "bq_in": a["L0_attn_bq"].reshape(1, -1),
        "bkv_in": np.concatenate([a["L0_attn_bk"], a["L0_attn_bv"]]).reshape(1, -1),
        "wq_in": a["L0_attn_Wq"].T.reshape(KC, P, CHUNKS, HID).transpose(0, 2, 1, 3).reshape(KC * CHUNKS, P, HID),
        "wo_in": a["L0_attn_Wo"].T.reshape(HEADS, P, HID),
        "wg_in": a["L0_ffn_wg"].T,
        "w13_in": w_13.reshape(EXPERTS, KC, P, UP).transpose(0, 2, 1, 3).reshape(EXPERTS, P, W13),
        "w2_in": a["L0_ffn_w2"],
    }
    arrays = {k: np.ascontiguousarray(v) for k, v in arrays.items()}
    nc = bacc.Bacc("TRN2", target_bir_lowering=False, num_devices=1)
    args = [nc.dram_tensor(k, v.shape, mybir.dt.from_np(v.dtype), kind="ExternalInput").ap() for k, v in arrays.items()]
    out = nc.dram_tensor("out", (TOKENS, HID), mybir.dt.float32, kind="ExternalOutput").ap()
    x, wkv, bq, bkv, wq, wo, wg, w13, w2 = args
    layer(nc, x, wkv, bq, bkv, wq, wo, wg, w13, w2, out)
    got = run_bass_kernel_spmd(nc, [arrays], core_ids=[0]).results[0]["out"]
    return got.reshape(BATCH, SEQ, HID)
```
